# Optimizing a Trainium2 kernel written in Bass

```python
import numpy as np
import jax
import jax.numpy as jnp

def _softmax(x, axis=-1):
    return jax.nn.softmax(x, axis=axis)

def _gelu(x):
    return jax.nn.gelu(x, approximate=True)

def _silu(x):
    return jax.nn.silu(x)

def _sigmoid(x):
    return jax.nn.sigmoid(x)

def _layernorm(x, axis=-1, eps=1e-05):
    m = jnp.mean(x, axis=axis, keepdims=True)
    v = jnp.var(x, axis=axis, keepdims=True)
    return (x - m) / jnp.sqrt(v + eps)

def _scatter_add(tgt, idx, src, axis=0):
    return tgt.at[idx].add(src)

def _segment_sum(src, seg, n):
    return jax.ops.segment_sum(src, seg, n)
kernel_name = 'mk_adj_preln_d1_adj_r2_3fd27f'

def setup_inputs(seed: int=0):
    np.random.seed(seed)
    _w = jnp.asarray

    def _rec_inputs():
        import jax
        import jax.numpy as jnp
        _gk = jax.random.key(seed)
        x = -9.29e-06 + 0.01 * jax.random.normal(jax.random.fold_in(_gk, 1), (8192, 128), jnp.float32)
        _a = jax.random.bernoulli(jax.random.fold_in(_gk, 2), 0.000976562, (8192, 8192))
        _af = _a.astype(jnp.float32)
        adj = _af
        return (x, adj)
    x, adj = _rec_inputs()

    def _L0_gnn_setup():
        import jax, jax.numpy as jnp
        import numpy as np
        N = 2048
        IN_C = 128
        OUT_C = 128
        H = 4
        D = OUT_C // H
        C_CURV = 1.0
        EPS = 1e-15
        MAX_TANH_ARG = 1.0 - 1e-05
        NEG_INF = -1e+30

        def logmap0(x, c):
            sqrt_c = jnp.sqrt(c)
            xn = jnp.maximum(jnp.linalg.norm(x, axis=-1, keepdims=True), EPS)
            arg = jnp.minimum(sqrt_c * xn, MAX_TANH_ARG)
            return jnp.arctanh(arg) * x / (sqrt_c * xn)

        def expmap0(v, c):
            sqrt_c = jnp.sqrt(c)
            vn = jnp.maximum(jnp.linalg.norm(v, axis=-1, keepdims=True), EPS)
            return jnp.tanh(sqrt_c * vn) * v / (sqrt_c * vn)
        key = jax.random.key(seed)
        k_x, k_adj, k_w, k_al, k_ar = jax.random.split(key, 5)
        x = 0.01 * jax.random.normal(k_x, (N, IN_C), dtype=jnp.float32)
        adj = (jax.random.uniform(k_adj, (N, N)) < 0.004).astype(jnp.float32)
        lim_w = float(np.sqrt(6.0 / (IN_C + OUT_C)))
        W = jax.random.uniform(k_w, (OUT_C, IN_C), minval=-lim_w, maxval=lim_w, dtype=jnp.float32)
        lim_a = float(np.sqrt(6.0 / (H + D)))
        a_l = jax.random.uniform(k_al, (H, D), minval=-lim_a, maxval=lim_a, dtype=jnp.float32)
        a_r = jax.random.uniform(k_ar, (H, D), minval=-lim_a, maxval=lim_a, dtype=jnp.float32)
        bias = jnp.zeros((OUT_C,), dtype=jnp.float32)
        return {'x': x, 'adj': adj, 'W': W, 'a_l': a_l, 'a_r': a_r, 'bias': bias}
    _L0_gnn_all = _L0_gnn_setup()
    _L0_gnn_in = {k: v for k, v in _L0_gnn_all.items() if k in ('W', 'a_l', 'a_r', 'bias')}
    del _L0_gnn_all
    return {'x': x, 'adj': adj, 'L0_gnn_W': _L0_gnn_in['W'], 'L0_gnn_a_l': _L0_gnn_in['a_l'], 'L0_gnn_a_r': _L0_gnn_in['a_r'], 'L0_gnn_bias': _L0_gnn_in['bias']}

def reference(x, adj, L0_gnn_W, L0_gnn_a_l, L0_gnn_a_r, L0_gnn_bias):
    import jax
    import jax.numpy as jnp

    def _L0_gnn_ref(x, adj, W, a_l, a_r, bias):
        import jax, jax.numpy as jnp
        import numpy as np
        N = 2048
        IN_C = 128
        OUT_C = 128
        H = 4
        D = OUT_C // H
        C_CURV = 1.0
        EPS = 1e-15
        MAX_TANH_ARG = 1.0 - 1e-05
        NEG_INF = -1e+30

        def logmap0(x, c):
            sqrt_c = jnp.sqrt(c)
            xn = jnp.maximum(jnp.linalg.norm(x, axis=-1, keepdims=True), EPS)
            arg = jnp.minimum(sqrt_c * xn, MAX_TANH_ARG)
            return jnp.arctanh(arg) * x / (sqrt_c * xn)

        def expmap0(v, c):
            sqrt_c = jnp.sqrt(c)
            vn = jnp.maximum(jnp.linalg.norm(v, axis=-1, keepdims=True), EPS)
            return jnp.tanh(sqrt_c * vn) * v / (sqrt_c * vn)
        n = x.shape[0]
        x_tan = logmap0(x, C_CURV)
        h = (x_tan @ W.T).reshape(n, H, D)
        e_l = jnp.einsum('nhd,hd->nh', h, a_l)
        e_r = jnp.einsum('nhd,hd->nh', h, a_r)
        logits = e_l[:, None, :] + e_r[None, :, :]
        logits = jax.nn.leaky_relu(logits, negative_slope=0.2)
        adj_hat = adj + jnp.eye(n, dtype=adj.dtype)
        mask = (adj_hat > 0)[:, :, None]
        logits = jnp.where(mask, logits, NEG_INF)
        attn = jax.nn.softmax(logits, axis=1)
        out = jnp.einsum('ijh,jhd->ihd', attn, h).reshape(n, -1)
        out = out + bias
        out = jax.nn.silu(out)
        return expmap0(out, C_CURV)
    h = jnp.maximum(_layernorm(x, axis=-1), 0.0)
    x = x + _L0_gnn_ref(h, adj, L0_gnn_W, L0_gnn_a_l, L0_gnn_a_r, L0_gnn_bias)
    return x

_drawn_inputs = setup_inputs


def setup_inputs(seed=0):
    import zlib

    import numpy as np

    out = dict(_drawn_inputs(seed))
    spreads = {'L0_gnn_bias': (0.0, 0.1)}
    factors = {}
    for name, (base, spread) in spreads.items():
        noise = np.random.default_rng([zlib.crc32(name.encode()), seed]).standard_normal(out[name].shape)
        drawn = base * np.exp(spread * noise) if base else spread * noise
        out[name] = jnp.asarray(drawn.astype(out[name].dtype))
    for name, factor in factors.items():
        out[name] = (out[name] * factor).astype(out[name].dtype)
    return out
```

```python
from contextlib import ExitStack

import concourse.bass as bass
from concourse import mybir

P = 128
ALU = mybir.AluOpType
ACT = mybir.ActivationFunctionType
AX = mybir.AxisListType.X
F32 = mybir.dt.float32
BF16 = mybir.dt.bfloat16
I32 = mybir.dt.int32
U32 = mybir.dt.uint32

HEADS = 4
BITS = 8
SEG = 64
SLOTS = 24
ROUNDS = SLOTS // 8
PEEL = 3
CHUNK = 2048
MAX_TANH_ARG = 1.0 - 1e-05
EPS_LN = 1e-05
EPS_NORM = 1e-15
NEG = -1e30


class Steps:

    def __init__(self, eng, sem, base=0, apart=False):
        self.eng, self.sem, self.base, self.n, self.apart = eng, sem, base, 0, apart

    def done(self, ins):
        self.n += 1
        ins.then_inc(self.sem, 1)

    def wait(self):
        self.eng.wait_ge(self.sem, self.base + self.n)
        if self.apart:
            self.eng.nop(nofuse=True)


def build(nc, x, adj, W, a_l, a_r, bias, ident_d, packw_d, posrow_d, onesrow_d, selfid_d, headsel_d, colid_d, out):
    N, D = x.shape
    T = N // P
    PAIRS = T // 2
    WORDS = N // BITS
    NCH = N // CHUNK
    BPC = CHUNK // WORDS
    NSEG = WORDS // SEG
    CANDS = NSEG * 8
    HD = D // HEADS
    ROW = D + HEADS
    RW = ROW + HEADS
    PIECE = 16
    NPIECE = T // PIECE
    QUADS = T // 4
    EXPO = 127 * WORDS
    ENTRIES = PEEL * SLOTS
    N_EXT, N_DEC, N_ATT, N_POST = 2 * ROUNDS, 37, 8, 4

    table = nc.dram_tensor("table", (N, ROW), F32, kind="Internal").ap()

    with ExitStack() as ctx:
        def sb(name, shape, dt=F32):
            return ctx.enter_context(nc.sbuf_tensor(name, shape, dt))

        def ps(name, shape, dt=F32):
            return ctx.enter_context(nc.psum_tensor(name, shape, dt))

        def sem(name):
            return ctx.enter_context(nc.semaphore(name))

        ident = sb("ident", [P, P])
        packw = sb("packw", [P, BITS, P], BF16)
        posrow = sb("posrow", [3, WORDS], BF16)
        onesrow = sb("onesrow", [3, P], BF16)
        selfid = sb("selfid", [P, T])
        headsel = sb("headsel", [P, HEADS])
        biasb = sb("biasb", [P, D])
        neg_tiny = sb("neg_tiny", [P, 1])
        wraw = sb("wraw", [P, D])
        acol = sb("acol", [P, 2])
        ablk = sb("ablk", [P, 2 * HEADS])
        waug = sb("waug", [P, RW])
        X = sb("X", [P, T, D])
        H = sb("H", [P, T, RW])
        adjbuf = sb("adjbuf", [P, 2, NCH, CHUNK])
        signs = sb("signs", [P, NCH, CHUNK], BF16)
        G = sb("G", [P, 2, SLOTS, ROW])
        mean = sb("mean", [P, T])
        stat = sb("stat", [P, 2, T])
        root = sb("root", [P, 2, T])
        sm = sb("sm", [P, 8, T])
        rT = sb("rT", [P, 2, 512])
        cand = sb("cand", [P, CANDS])
        cand2 = sb("cand2", [P, CANDS])
        words = sb("words", [P, 2, SLOTS])
        keyi = sb("keyi", [P, 2, SLOTS], I32)
        posi = sb("posi", [P, 2, SLOTS], I32)
        wi = sb("wi", [P, 2, SLOTS], I32)
        wf = sb("wf", [P, 2, SLOTS])
        topbit = sb("topbit", [P, 2, SLOTS], I32)
        bitno = sb("bitno", [P, 2, SLOTS], I32)
        ents = sb("ents", [P, 2, ENTRIES])
        notself = sb("notself", [P, 2, ENTRIES])
        ents2 = sb("ents2", [P, 2, ENTRIES])
        top = sb("top", [P, 2, SLOTS])
        topc = sb("topc", [P, 2, SLOTS])
        inv = sb("inv", [P, 2, SLOTS])
        idxf = sb("idxf", [P, 2, SLOTS])
        idx = sb("idx", [P, 2, 2, SLOTS], U32)
        pen = sb("pen", [P, 2, 2, SLOTS])
        over4 = sb("over4", [P, 2, 4])
        over = sb("over", [P, T])
        lg = sb("lg", [P, 2, SLOTS + 1, HEADS])
        prob = sb("prob", [P, 2, SLOTS + 1, HEADS])
        rowmax = sb("rowmax", [P, HEADS])
        den = sb("den", [P, HEADS])
        rden = sb("rden", [P, 2, HEADS])
        selfp = sb("selfp", [P, 2, D])
        o = sb("o", [P, 2, D])
        eo = sb("eo", [P, 2, D])
        sq = sb("sq", [P, 2, D])
        nrm = sb("nrm", [P, T])

        ones = sb("ones", [P, 1])
        rowflag = sb("rowflag", [P, T])
        flagrow = sb("flagrow", [1, T])
        anyflag = sb("anyflag", [1, 1])
        anyi = sb("anyi", [1, 1], I32)
        tally = sb("tally", [1, T + 1, 2])
        ctl = sb("ctl", [1, T, 3], I32)
        degree = sb("degree", [P, 1])
        maxdeg = sb("maxdeg", [1, 1])
        degi = sb("degi", [1, 1], I32)
        rounds = sb("rounds", [1, T], I32)
        top8 = sb("top8", [P, 8])
        topc8 = sb("topc8", [P, 8])
        inv8 = sb("inv8", [P, 8])
        idxf8 = sb("idxf8", [P, 8])
        idx8 = sb("idx8", [P, 8], U32)
        pen8 = sb("pen8", [P, 8])
        lg8 = sb("lg8", [P, 9, HEADS])
        prob8 = sb("prob8", [P, 9, HEADS])
        newmax = sb("newmax", [P, HEADS])
        oldmax = sb("oldmax", [P, HEADS])
        rmax8 = sb("rmax8", [P, HEADS])
        den8 = sb("den8", [P, HEADS])
        sum8 = sb("sum8", [P, HEADS])
        acc = sb("acc", [P, D])
        part = sb("part", [P, D])

        keys = ps("keys", [P, 2, WORDS])
        po = ps("po", [P, 2, 512])
        pt = ps("pt", [P, 2, 512])

        x_landed = [sem(f"x_landed{i}") for i in range(NPIECE)]
        w_landed = sem("w_landed")
        const_landed = sem("const_landed")
        adj_landed = [sem(f"adj_landed{i}") for i in range(2 * NCH)]
        cleared = sem("cleared")
        tiny_set = sem("tiny_set")
        w_turned = sem("w_turned")
        a_spread = sem("a_spread")
        waug_ready = sem("waug_ready")
        centred = sem("centred")
        squared = sem("squared")
        relu_ready = sem("relu_ready")
        sq_read = sem("sq_read")
        turned = sem("turned")
        rT_ready = sem("rT_ready")
        h_done = sem("h_done")
        h_read = sem("h_read")
        prep_step = sem("prep_step")
        stat_ready = sem("stat_ready")
        root_ready = sem("root_ready")
        arg_ready = sem("arg_ready")
        logs_ready = sem("logs_ready")
        scaled = sem("scaled")
        table_stored = sem("table_stored")
        signed = sem("signed")
        packed = sem("packed")
        keys_read = sem("keys_read")
        ext_step = sem("ext_step")
        dec_step = sem("dec_step")
        lists_ready = sem("lists_ready")
        gathered = [sem("gathered0"), sem("gathered1")]
        att_step = sem("att_step")
        logits_ready = sem("logits_ready")
        probs_ready = sem("probs_ready")
        weighted = sem("weighted")
        summed = sem("summed")
        sums_read = sem("sums_read")
        post_step = sem("post_step")
        o_ready = sem("o_ready")
        expo_ready = sem("expo_ready")
        z_ready = sem("z_ready")
        norms_rooted = sem("norms_rooted")
        norms_kept = sem("norms_kept")
        tanh_ready = sem("tanh_ready")
        fin_step = sem("fin_step")
        flags_step = sem("flags_step")
        flags_counted = sem("flags_counted")
        any_ready = sem("any_ready")
        ctl_ready = sem("ctl_ready")
        colid_landed = sem("colid_landed")
        slow_free = sem("slow_free")
        slow_adj = sem("slow_adj")
        slow_step = sem("slow_step")
        degrees_ready = sem("degrees_ready")
        degrees_turned = sem("degrees_turned")
        rounds_ready = sem("rounds_ready")
        round_step = sem("round_step")
        round_lists = sem("round_lists")
        round_gathered = sem("round_gathered")
        round_logits = sem("round_logits")
        round_probs = sem("round_probs")
        slow_o = sem("slow_o")
        slow_expo = sem("slow_expo")
        main_done = sem("main_done")
        tally_step = sem("tally_step")
        slow_done = sem("slow_done")
        out_ready = sem("out_ready")
        out_stored = sem("out_stored")

        Gflat = G[:, :, :, :].rearrange("p b k r -> p (b k r)")
        SPAN = PIECE * D

        def centred_piece(b):
            return Gflat[:, b * SPAN:(b + 1) * SPAN].rearrange("p (t c) -> p t c", c=D)

        squares = Gflat[:, 2 * SPAN:3 * SPAN].rearrange("p (t c) -> p t c", c=D)
        x_t = x.rearrange("(t p) c -> p t c", p=P)
        out_t = out.rearrange("(t p) c -> p t c", p=P)
        table_t = table.rearrange("(t p) c -> p t c", p=P)

        def along(ap, n):
            return ap.unsqueeze(2).broadcast_to([ap.shape[0], ap.shape[1], n])

        colid = adjbuf[:, 1, :, :].rearrange("p c n -> p (c n)")
        slow_keys = adjbuf[:, 0, :, :].rearrange("p c n -> p (c n)")
        slow_own = G[:, 1, 0, :]
        MAXROUNDS = N // 8

        def any_flagged(eng):
            eng.wait_ge(any_ready, 1)
            eng.nop(nofuse=True)
            return eng.value_load(anyi[0:1, 0:1], min_val=0, max_val=T)

        def control(eng, t):
            eng.wait_ge(ctl_ready, t + 1)
            eng.nop(nofuse=True)
            flag = eng.value_load(ctl[0:1, bass.ds(t, 1), 0], min_val=0, max_val=1)
            rank = eng.value_load(ctl[0:1, bass.ds(t, 1), 1], min_val=0, max_val=T)
            base = eng.value_load(ctl[0:1, bass.ds(t, 1), 2], min_val=0, max_val=T * MAXROUNDS)
            return flag, rank, base

        def round_count(eng, t, rank):
            eng.wait_ge(rounds_ready, rank + 1)
            eng.nop(nofuse=True)
            return eng.value_load(rounds[0:1, bass.ds(t, 1)], min_val=0, max_val=MAXROUNDS)

        block = ctx.enter_context(nc.Block())

        @block.sync
        def _(sp):
            def load_adj(t, b, c):
                sp.dma_start(adjbuf[:, b, c, :], adj[bass.ds(t * P, P), c * CHUNK:(c + 1) * CHUNK]) \
                    .then_inc(adj_landed[b * NCH + c], 16)

            for i in range(NPIECE):
                sp.dma_start(X[:, i * PIECE:(i + 1) * PIECE, :], x_t[:, i * PIECE:(i + 1) * PIECE, :]) \
                    .then_inc(x_landed[i], 16)
                if i == 0:
                    for dst, src in ((wraw[:, :], W), (acol[:, 0:1], a_r.rearrange("h (d u) -> (h d) u", u=1)),
                                     (acol[:, 1:2], a_l.rearrange("h (d u) -> (h d) u", u=1)),
                                     (ident[:, :], ident_d), (headsel[:, :], headsel_d)):
                        sp.dma_start(dst, src).then_inc(w_landed, 16)
            for dst, src in ((packw[:, :, :], packw_d), (posrow[:, :], posrow_d), (onesrow[:, :], onesrow_d),
                             (selfid[:, :], selfid_d),
                             (biasb[:, :], bias.unsqueeze(0).broadcast_to([P, D]))):
                sp.dma_start(dst, src).then_inc(const_landed, 16)
            for t in range(2):
                for c in range(NCH):
                    load_adj(t, t, c)
            for i in range(NPIECE):
                sp.wait_ge(scaled, i + 1)
                sp.dma_start(table_t[:, i * PIECE:(i + 1) * PIECE, :], H[:, i * PIECE:(i + 1) * PIECE, 0:ROW]) \
                    .then_inc(table_stored, 16)
            with sp.Fori(1, PAIRS) as pair:
                for b in range(2):
                    for c in range(NCH):
                        sp.wait_ge(signed, pair * (2 * NCH) + (b * NCH + c + 1 - 2 * NCH))
                        load_adj(pair * 2 + b, b, c)
            with sp.If(any_flagged(sp) > 0):
                sp.dma_start(colid, colid_d.broadcast_to([P, N])).then_inc(colid_landed, 16)
                with sp.Fori(0, T) as t:
                    flag, rank, _ = control(sp, t)
                    with sp.If(flag > 0):
                        sp.wait_ge(slow_free, rank + 1)
                        sp.dma_start(slow_keys, adj[bass.ds(t * P, P), :]).then_inc(slow_adj, 16)
                        sp.dma_start(slow_own, table[bass.ds(t * P, P), :]).then_inc(slow_adj, 16)
            for i in range(NPIECE):
                sp.wait_ge(out_ready, i + 1)
                sp.dma_start(out_t[:, i * PIECE:(i + 1) * PIECE, :], X[:, i * PIECE:(i + 1) * PIECE, :]) \
                    .then_inc(out_stored, 16)
            sp.wait_ge(out_stored, 16 * NPIECE)

        @block.gpsimd
        def _(pool):
            nc.gpsimd.memset(Gflat[:, :], 0.0).then_inc(cleared, 1)
            pool.wait_ge(table_stored, 16 * NPIECE)

            def gather(pair, q, first):
                pool.wait_ge(lists_ready, pair + 1)
                for b in range(2):
                    if not first:
                        pool.wait_ge(summed, pair * 2 + (b - 1))
                    pool.nop(nofuse=True)
                    for k in range(SLOTS):
                        nc.gpsimd.indirect_dma_start(
                            G[:, b, k, :], None, table,
                            bass.IndirectOffsetOnAxis(ap=idx[:, q, b, k:k + 1], axis=0),
                            bounds_check=N - 1, oob_is_err=False).then_inc(gathered[b], 16)

            gather(0, 0, True)
            with pool.Fori(0, PAIRS // 2 - 1) as i:
                gather(i * 2 + 1, 1, False)
                gather(i * 2 + 2, 0, False)
            gather(PAIRS - 1, 1, False)

            with pool.If(any_flagged(pool) > 0):
                with pool.Fori(0, T) as t:
                    flag, rank, base = control(pool, t)
                    with pool.If(flag > 0):
                        count = round_count(pool, t, rank)
                        with pool.Fori(0, MAXROUNDS) as r:
                            with pool.If(r < count):
                                pool.wait_ge(round_lists, base + r + 1)
                                pool.nop(nofuse=True)
                                for k in range(8):
                                    nc.gpsimd.indirect_dma_start(
                                        G[:, 0, k, :], None, table,
                                        bass.IndirectOffsetOnAxis(ap=idx8[:, k:k + 1], axis=0),
                                        bounds_check=N - 1, oob_is_err=False).then_inc(round_gathered, 16)

        @block.scalar
        def _(act):
            def keep(quad):
                act.wait_ge(h_done, quad + 1)
                for j in range(2):
                    last = nc.scalar.copy(H[:, 4 * quad + 2 * j:4 * quad + 2 * j + 2, :],
                                          po[:, j, 0:2 * RW].rearrange("p (t c) -> p t c", c=RW))
                last.then_inc(h_read, 1)

            for i in range(NPIECE):
                act.wait_ge(centred, i + 1)
                if i:
                    act.wait_ge(sq_read, 2 * i)
                else:
                    act.wait_ge(cleared, 1)
                nc.scalar.activation(squares, centred_piece(i % 2), ACT.Square).then_inc(squared, 1)
                act.wait_ge(relu_ready, i + 1)
                act.wait_ge(sq_read, 2 * i + 1)
                nc.scalar.activation(squares, centred_piece(i % 2), ACT.Square).then_inc(squared, 1)
                for j in range(PIECE // 4):
                    quad = i * (PIECE // 4) + j
                    act.wait_ge(turned, quad + 1)
                    if quad >= 2:
                        act.wait_ge(h_done, quad - 1)
                    nc.scalar.copy(rT[:, quad % 2, :], pt[:, quad % 2, :]).then_inc(rT_ready, 1)
                    if quad:
                        keep(quad - 1)
            keep(QUADS - 1)
            act.wait_ge(stat_ready, 1)
            nc.scalar.activation(root[:, :, :], stat[:, :, :], ACT.Sqrt).then_inc(root_ready, 1)
            act.wait_ge(arg_ready, 1)
            nc.scalar.activation(sm[:, 2, :], sm[:, 1, :], ACT.Ln, bias=1.0, scale=1.0).then_inc(logs_ready, 1)
            nc.scalar.activation(sm[:, 3, :], sm[:, 1, :], ACT.Ln, bias=1.0, scale=-1.0).then_inc(logs_ready, 1)

            def sign(pair, first):
                for b in range(2):
                    for c in range(NCH):
                        act.wait_ge(adj_landed[b * NCH + c], pair * 16 + 16)
                        if b or not first:
                            act.wait_ge(packed, pair * (2 * NCH) + ((b - 1) * NCH + c + 1))
                        nc.scalar.activation(signs[:, c, :], adjbuf[:, b, c, :], ACT.Sign, bias=neg_tiny[:, :]) \
                            .then_inc(signed, 1)

            def exps(pair):
                for b in range(2):
                    act.wait_ge(logits_ready, pair * 2 + (b + 1))
                    nc.scalar.activation(prob[:, b, :, :], lg[:, b, :, :], ACT.Exp).then_inc(probs_ready, 1)
                act.wait_ge(o_ready, pair + 1)
                nc.scalar.activation(eo[:, :, :], o[:, :, :], ACT.Exp, scale=-1.0).then_inc(expo_ready, 1)

            act.wait_ge(tiny_set, 1)
            sign(0, True)
            with act.Fori(0, PAIRS - 1) as i:
                sign(i + 1, False)
                exps(i)
            exps(PAIRS - 1)
            with act.If(any_flagged(act) > 0):
                with act.Fori(0, T) as t:
                    flag, rank, base = control(act, t)
                    with act.If(flag > 0):
                        count = round_count(act, t, rank)
                        with act.Fori(0, MAXROUNDS) as r:
                            with act.If(r < count):
                                act.wait_ge(round_logits, base + r + 1)
                                nc.scalar.activation(prob8[:, :, :], lg8[:, :, :], ACT.Exp).then_inc(round_probs, 1)
                        act.wait_ge(slow_o, rank + 1)
                        nc.scalar.activation(eo[:, 0, :], o[:, 0, :], ACT.Exp, scale=-1.0).then_inc(slow_expo, 1)
            act.wait_ge(slow_done, 1)
            nc.scalar.activation(sm[:, 0, :], nrm[:, :], ACT.Sqrt).then_inc(norms_rooted, 1)
            act.wait_ge(norms_kept, 1)
            nc.scalar.activation(sm[:, 2, :], sm[:, 1, :], ACT.Tanh).then_inc(tanh_ready, 1)

        @block.tensor
        def _(pe):
            pe.wait_ge(w_landed, 16 * 5)
            nc.tensor.transpose(pt[:, 0, 0:P], wraw[:, :], ident[:, :]).then_inc(w_turned, 1)
            pe.wait_ge(a_spread, 1)
            nc.tensor.matmul(pt[:, 1, 0:2 * HEADS], wraw[:, :], ablk[:, :], start=True, stop=True) \
                .then_inc(w_turned, 1)
            pe.wait_ge(waug_ready, 1)

            def turn(quad, b, first):
                pe.wait_ge(relu_ready, quad // (PIECE // 4) + 1)
                if not first:
                    pe.wait_ge(rT_ready, quad - 1)
                for j in range(4):
                    tt = (quad % (PIECE // 4)) * 4 + j
                    last = nc.tensor.transpose(pt[:, b, j * P:(j + 1) * P],
                                               centred_piece(quad // (PIECE // 4) % 2)[:, tt, :], ident[:, :])
                last.then_inc(turned, 1)

            def project(quad, b):
                pe.wait_ge(rT_ready, quad + 1)
                if quad:
                    pe.wait_ge(h_read, quad)
                for j in range(4):
                    last = nc.tensor.matmul(po[:, j // 2, (j % 2) * RW:(j % 2 + 1) * RW],
                                            rT[:, b, j * P:(j + 1) * P], waug[:, :], start=True, stop=True)
                last.then_inc(h_done, 1)

            turn(0, 0, True)
            for quad in range(QUADS):
                if quad + 1 < QUADS:
                    turn(quad + 1, (quad + 1) % 2, quad + 1 < 2)
                project(quad, quad % 2)

            def pack(pair, first):
                for b in range(2):
                    if not first:
                        pe.wait_ge(keys_read, pair * 2 + (b - 1))
                    for half in range(WORDS // 512):
                        nc.tensor.matmul(keys[:, b, half * 512:(half + 1) * 512], onesrow[:, :],
                                         posrow[:, half * 512:(half + 1) * 512], start=True, stop=False)
                    for c in range(NCH):
                        pe.wait_ge(signed, pair * (2 * NCH) + (b * NCH + c + 1))
                        for k in range(BPC):
                            for half in range(WORDS // 512):
                                at = k * WORDS + half * 512
                                last = nc.tensor.matmul(keys[:, b, half * 512:(half + 1) * 512],
                                                        packw[:, c * BPC + k, :], signs[:, c, at:at + 512],
                                                        start=False, stop=(c * BPC + k == BITS - 1))
                        last.then_inc(packed, 1)

            def sums(pair, first):
                for b in range(2):
                    pe.wait_ge(weighted, pair * 2 + (b + 1))
                    if not first and b == 0:
                        pe.wait_ge(sums_read, pair)
                    for k in range(SLOTS):
                        nc.tensor.matmul(po[:, b, 0:D], ident[:, :], G[:, b, k, 0:D], start=(k == 0), stop=False)
                    nc.tensor.matmul(po[:, b, 0:D], ident[:, :], selfp[:, b, :], start=False, stop=True) \
                        .then_inc(summed, 1)

            pe.wait_ge(const_landed, 16 * 5)
            pack(0, True)
            pack(1, False)
            pe.wait_ge(h_read, QUADS)
            sums(0, True)
            with pe.Fori(1, PAIRS - 1) as i:
                pack(i + 1, False)
                sums(i, False)
            sums(PAIRS - 1, False)

            pe.wait_ge(main_done, 1)
            nc.tensor.matmul(po[0:1, 0, 0:T], ones[:, :], rowflag[:, :], start=True, stop=True) \
                .then_inc(flags_counted, 1)
            with pe.If(any_flagged(pe) > 0):
                with pe.Fori(0, T) as t:
                    flag, rank, _ = control(pe, t)
                    with pe.If(flag > 0):
                        pe.wait_ge(degrees_ready, rank + 1)
                        nc.tensor.matmul(po[0:1, 1, 0:P], degree[:, :], ident[:, :], start=True, stop=True) \
                            .then_inc(degrees_turned, 1)

        @block.vector
        def _(dve):
            V = nc.vector
            V.memset(neg_tiny[:, :], -1.1754944e-38).then_inc(tiny_set, 1)
            st = Steps(dve, prep_step)
            dve.wait_ge(w_landed, 16 * 5)
            V.tensor_scalar(ablk[:, 0:HEADS], headsel[:, :], acol[:, 0:1], None, ALU.mult)
            V.tensor_scalar(ablk[:, HEADS:2 * HEADS], headsel[:, :], acol[:, 1:2], None, ALU.mult) \
                .then_inc(a_spread, 1)
            dve.wait_ge(w_turned, 2)
            V.tensor_copy(waug[:, 0:D], pt[:, 0, 0:P])
            V.tensor_copy(waug[:, D:RW], pt[:, 1, 0:2 * HEADS]).then_inc(waug_ready, 1)
            dve.wait_ge(cleared, 1)

            def stats(i):
                here = slice(i * PIECE, (i + 1) * PIECE)
                dve.wait_ge(x_landed[i], 16)
                st.done(V.tensor_reduce(mean[:, here], X[:, here, :], AX, ALU.add))
                st.wait()
                st.done(V.tensor_scalar(mean[:, here], mean[:, here], 1.0 / D, None, ALU.mult))
                st.wait()
                piece = centred_piece(i % 2)
                if i >= 2:
                    dve.wait_ge(turned, (i - 1) * (PIECE // 4))
                V.tensor_tensor(piece, X[:, here, :], along(mean[:, here], D), ALU.subtract).then_inc(centred, 1)
                dve.wait_ge(squared, 2 * i + 1)
                V.tensor_reduce(stat[:, 0, here], squares, AX, ALU.add).then_inc(sq_read, 1)
                V.tensor_scalar(piece, piece, 0.0, None, ALU.max).then_inc(relu_ready, 1)
                dve.wait_ge(squared, 2 * i + 2)
                V.tensor_reduce(stat[:, 1, here], squares, AX, ALU.add).then_inc(sq_read, 1)

            for i in range(NPIECE):
                stats(i)

            def small(ins):
                st.done(ins)
                st.wait()

            dve.wait_ge(sq_read, 2 * NPIECE)
            V.tensor_scalar(stat[:, 0, :], stat[:, 0, :], 1.0 / D, EPS_LN, ALU.mult, ALU.add).then_inc(stat_ready, 1)
            dve.wait_ge(root_ready, 1)
            rstd, arg, lp, lm, n, a2, poly, tmp = root[:, 0, :], sm[:, 1, :], sm[:, 2, :], sm[:, 3, :], sm[:, 0, :], sm[:, 4, :], sm[:, 5, :], sm[:, 6, :]
            small(V.reciprocal(rstd, rstd))
            small(V.tensor_tensor(n, root[:, 1, :], rstd, ALU.mult))
            small(V.tensor_scalar(n, n, EPS_NORM, None, ALU.max))
            V.tensor_scalar(arg, n, MAX_TANH_ARG, None, ALU.min).then_inc(arg_ready, 1)
            dve.wait_ge(arg_ready, 1)
            small(V.tensor_tensor(a2, arg, arg, ALU.mult))
            small(V.tensor_scalar(poly, a2, 1.0 / 9, 1.0 / 7, ALU.mult, ALU.add))
            for c in (1.0 / 5, 1.0 / 3, 1.0):
                small(V.tensor_tensor(poly, poly, a2, ALU.mult))
                small(V.tensor_scalar(poly, poly, c, None, ALU.add))
            small(V.tensor_tensor(poly, poly, arg, ALU.mult))
            dve.wait_ge(logs_ready, 2)
            small(V.tensor_tensor(lp, lp, lm, ALU.subtract))
            small(V.tensor_scalar(lp, lp, 0.5, None, ALU.mult))
            small(V.tensor_tensor(poly, poly, lp, ALU.subtract))
            small(V.tensor_scalar(tmp, arg, 0.1, None, ALU.is_lt))
            small(V.tensor_tensor(poly, poly, tmp, ALU.mult))
            small(V.tensor_tensor(lp, lp, poly, ALU.add))
            small(V.reciprocal(n, n))
            small(V.tensor_tensor(lp, lp, n, ALU.mult))
            small(V.tensor_tensor(lp, lp, rstd, ALU.mult))
            dve.wait_ge(h_read, QUADS)
            for i in range(NPIECE):
                here = slice(i * PIECE, (i + 1) * PIECE)
                V.tensor_tensor(H[:, here, :], H[:, here, :], along(lp[:, here], RW), ALU.mult).then_inc(scaled, 1)
            dve.wait_ge(scaled, NPIECE)
            dve.wait_ge(const_landed, 16 * 5)

            def topk(steps, dst, src, spare, imm):
                for r in range(ROUNDS):
                    if r:
                        steps.wait()
                    dve.nop(nofuse=True)
                    steps.done(V.max(dst[:, 8 * r:8 * r + 8], src))
                    if r < ROUNDS - 1:
                        steps.wait()
                        dve.nop(nofuse=True)
                        steps.done(V.match_replace(spare, dst[:, 8 * r:8 * r + 8], src, imm))
                        src = spare

            def extract(t, b):
                ext = Steps(dve, ext_step, t * N_EXT)
                dve.wait_ge(packed, t * NCH + NCH)
                dve.nop(nofuse=True)
                for s in range(NSEG):
                    last = V.max(cand[:, 8 * s:8 * s + 8], keys[:, b, s * SEG:(s + 1) * SEG])
                last.then_inc(keys_read, 1)
                dve.wait_ge(keys_read, t + 1)
                ext.done(V.tensor_reduce(over4[:, b, 0:1], cand[:, 7:CANDS:8], AX, ALU.max))
                topk(ext, words[:, b, :], cand[:, :], cand2[:, :], -1.0)
                assert ext.n == N_EXT
                ext.wait()

            def decode(pair, q):
                dec = Steps(dve, dec_step, pair * N_DEC)

                def step(ins):
                    dec.done(ins)
                    dec.wait()

                step(V.tensor_scalar(keyi[:, :, :], words[:, :, :], float(WORDS), None, ALU.mult))
                dec.done(V.tensor_scalar(posi[:, :, :], keyi[:, :, :], WORDS - 1, None, ALU.bitwise_and))
                step(V.tensor_scalar(wi[:, :, :], keyi[:, :, :], WORDS.bit_length() - 1, None,
                                     ALU.logical_shift_right))
                step(V.tensor_copy(wf[:, :, :], wi[:, :, :]))
                for r in range(PEEL):
                    bits = wf[:, :, :].bitcast(I32)
                    dec.done(V.tensor_scalar(topbit[:, :, :], bits, 0x7F800000, None, ALU.bitwise_and))
                    step(V.tensor_scalar(bitno[:, :, :], bits, 23, WORDS.bit_length() - 1,
                                         ALU.logical_shift_right, ALU.logical_shift_left))
                    dec.done(V.tensor_tensor(ents[:, :, r * SLOTS:(r + 1) * SLOTS], bitno[:, :, :], posi[:, :, :],
                                             ALU.add))
                    step(V.tensor_tensor(wf[:, :, :], wf[:, :, :], topbit[:, :, :].bitcast(F32), ALU.subtract))
                own = along(selfid[:, bass.ds(pair * 2, 2)], ENTRIES)
                step(V.tensor_scalar(ents[:, :, :], ents[:, :, :], 1.0 - EXPO, None, ALU.add))
                step(V.tensor_tensor(notself[:, :, :], ents[:, :, :], own, ALU.not_equal))
                step(V.tensor_tensor(ents[:, :, :], ents[:, :, :], notself[:, :, :], ALU.mult))
                for b in range(2):
                    topk(dec, top[:, b, :], ents[:, b, :], ents2[:, b, :], -2.0 * EXPO)
                dec.done(V.tensor_reduce(over4[:, :, 2:3], wf[:, :, :], AX, ALU.max))
                dec.done(V.tensor_copy(over4[:, :, 1:2], words[:, :, SLOTS - 1:SLOTS]))
                dec.wait()
                dec.done(V.tensor_copy(over4[:, :, 3:4], top[:, :, SLOTS - 1:SLOTS]))
                dec.done(V.tensor_scalar(topc[:, :, :], top[:, :, :], 0.0, None, ALU.max))
                dec.done(V.tensor_scalar(inv[:, :, :], top[:, :, :], 0.5, None, ALU.is_lt))
                dec.wait()
                dec.done(V.tensor_reduce(over[:, bass.ds(pair * 2, 2)], over4[:, :, :], AX, ALU.max))
                dec.done(V.tensor_scalar(pen[:, q, :, :], inv[:, :, :], NEG, None, ALU.mult))
                step(V.scalar_tensor_tensor(idxf[:, :, :], inv[:, :, :], float(N + 1), topc[:, :, :], ALU.mult,
                                            ALU.add))
                V.tensor_scalar(idx[:, q, :, :], idxf[:, :, :], -1.0, None, ALU.add).then_inc(lists_ready, 1)
                return dec.n

            def attend(pair, q, b):
                t = pair * 2 + b
                att = Steps(dve, att_step, t * N_ATT)

                def step(ins):
                    att.done(ins)
                    att.wait()

                own = H[:, bass.ds(t, 1), :]
                e_l = H[:, bass.ds(t, 1), ROW:RW]
                dve.wait_ge(gathered[b], pair * (16 * SLOTS) + 16 * SLOTS)
                L = lg[:, b, :, :]
                att.done(V.tensor_tensor(L[:, 0:SLOTS, :], G[:, b, :, D:ROW],
                                         e_l.broadcast_to([P, SLOTS, HEADS]), ALU.add))
                step(V.tensor_tensor(L[:, SLOTS:SLOTS + 1, :], own[:, :, D:ROW], e_l, ALU.add))
                Lf = L.rearrange("p k h -> p (k h)")
                step(V.scalar_tensor_tensor(Lf, Lf, 0.2, Lf, ALU.mult, ALU.max))
                step(V.tensor_tensor(L[:, 0:SLOTS, :], L[:, 0:SLOTS, :], along(pen[:, q, b, :], HEADS), ALU.add))
                step(V.tensor_reduce(rowmax[:, :], L.rearrange("p k h -> p h k"), AX, ALU.max))
                V.tensor_tensor(L, L, rowmax[:, :].unsqueeze(1).broadcast_to([P, SLOTS + 1, HEADS]),
                                ALU.subtract).then_inc(logits_ready, 1)
                dve.wait_ge(probs_ready, pair * 2 + (b + 1))
                pr = prob[:, b, :, :]
                step(V.tensor_reduce(den[:, :], pr.rearrange("p k h -> p h k"), AX, ALU.add))
                att.done(V.reciprocal(rden[:, b, :], den[:, :]))
                rows = G[:, b, :, 0:D].rearrange("p k (h d) -> p k h d", h=HEADS)
                att.done(V.tensor_tensor(rows, rows, pr[:, 0:SLOTS, :].unsqueeze(3)
                                         .broadcast_to([P, SLOTS, HEADS, HD]), ALU.mult))
                V.tensor_tensor(selfp[:, b, :].rearrange("p (h d) -> p h d", h=HEADS),
                                own[:, 0, 0:D].rearrange("p (h d) -> p h d", h=HEADS),
                                along(pr[:, SLOTS, :], HD), ALU.mult).then_inc(weighted, 1)
                assert att.n == N_ATT, att.n

            def finish(pair):
                post = Steps(dve, post_step, pair * N_POST)

                def step(ins):
                    post.done(ins)
                    post.wait()

                dve.wait_ge(summed, pair * 2 + 2)
                V.tensor_tensor(o[:, :, :].rearrange("p b (h d) -> p b h d", h=HEADS),
                                po[:, :, 0:D].rearrange("p b (h d) -> p b h d", h=HEADS),
                                rden[:, :, :].unsqueeze(3).broadcast_to([P, 2, HEADS, HD]),
                                ALU.mult).then_inc(sums_read, 1)
                dve.wait_ge(sums_read, pair + 1)
                V.tensor_tensor(o[:, :, :], o[:, :, :], biasb[:, :].unsqueeze(1).broadcast_to([P, 2, D]),
                                ALU.add).then_inc(o_ready, 1)
                dve.wait_ge(expo_ready, pair + 1)
                step(V.tensor_scalar(eo[:, :, :], eo[:, :, :], 1.0, None, ALU.add))
                step(V.reciprocal(eo[:, :, :], eo[:, :, :]))
                z = H[:, bass.ds(pair * 2, 2), 0:D]
                step(V.tensor_tensor(z, o[:, :, :], eo[:, :, :], ALU.mult))
                step(V.tensor_tensor(sq[:, :, :], z, z, ALU.mult))
                V.tensor_reduce(nrm[:, bass.ds(pair * 2, 2)], sq[:, :, :], AX, ALU.add).then_inc(z_ready, 1)
                assert post.n == N_POST, post.n

            def neighbours(pair, q):
                extract(pair * 2, 0)
                extract(pair * 2 + 1, 1)
                n = decode(pair, q)
                assert n == N_DEC, n

            def aggregate(pair, q):
                attend(pair, q, 0)
                attend(pair, q, 1)
                finish(pair)

            neighbours(0, 0)
            with dve.Fori(0, PAIRS // 2 - 1) as i:
                neighbours(i * 2 + 1, 1)
                aggregate(i * 2, 0)
                neighbours(i * 2 + 2, 0)
                aggregate(i * 2 + 1, 1)
            neighbours(PAIRS - 1, 1)
            aggregate(PAIRS - 2, 0)
            aggregate(PAIRS - 1, 1)

            fl = Steps(dve, flags_step)

            def flagstep(ins):
                fl.done(ins)
                fl.wait()

            V.memset(ones[:, :], 1.0)
            V.tensor_scalar(rowflag[:, :], over[:, :], 1.0, None, ALU.is_ge).then_inc(main_done, 1)
            dve.wait_ge(flags_counted, 1)
            flagstep(V.tensor_scalar(flagrow[:, :], po[0:1, 0, 0:T], 0.5, None, ALU.is_gt))
            flagstep(V.tensor_reduce(anyflag[:, :], flagrow[:, :], AX, ALU.add))
            V.tensor_copy(anyi[:, :], anyflag[:, :]).then_inc(any_ready, 1)

            def slow_tile(t, rank, base):
                SLOW, ROUND = 12, 19
                sl = Steps(dve, slow_step, rank * SLOW, apart=True)

                def step(ins):
                    sl.done(ins)
                    sl.wait()

                heads = "p (h d) -> p h d"
                e_l = H[:, bass.ds(t, 1), ROW:RW]
                dve.wait_ge(slow_adj, rank * 32 + 32)
                step(V.scalar_tensor_tensor(slow_keys, slow_keys, 0.0, colid, ALU.is_gt, ALU.mult))
                step(V.scalar_tensor_tensor(slow_keys, colid, selfid[:, bass.ds(t, 1)], slow_keys, ALU.not_equal,
                                            ALU.mult))
                V.tensor_scalar(signs[:, :, :].rearrange("p c n -> p (c n)"), slow_keys, 0.5, None, ALU.is_gt,
                                ALU.add, accum_out=degree[:, :]).then_inc(degrees_ready, 1)
                dve.wait_ge(degrees_turned, rank + 1)
                step(V.tensor_reduce(maxdeg[:, :], po[0:1, 1, 0:P], AX, ALU.max))
                step(V.tensor_scalar(degi[:, :], maxdeg[:, :], 7.0, None, ALU.add))
                step(V.tensor_scalar(rounds[0:1, bass.ds(t, 1)], degi[:, :], 3, None, ALU.logical_shift_right))
                step(V.tensor_copy(maxdeg[:, :], rounds[0:1, bass.ds(t, 1)]))
                step(V.tensor_tensor(tally[0:1, bass.ds(t + 1, 1), 1], tally[0:1, bass.ds(t + 1, 1), 1], maxdeg[:, :],
                                     ALU.add))
                step(V.tensor_tensor(oldmax[:, :], slow_own[:, D:ROW], e_l[:, 0, :], ALU.add))
                step(V.scalar_tensor_tensor(oldmax[:, :], oldmax[:, :], 0.2, oldmax[:, :], ALU.mult, ALU.max))
                sl.done(V.memset(den8[:, :], 1.0))
                V.tensor_copy(acc[:, :], slow_own[:, 0:D]).then_inc(rounds_ready, 1)
                count = round_count(dve, t, rank)
                with dve.Fori(0, MAXROUNDS) as r:
                    with dve.If(r < count):
                        n = base + r
                        rs = Steps(dve, round_step, n * ROUND, apart=True)

                        def rstep(ins):
                            rs.done(ins)
                            rs.wait()

                        rstep(V.max(top8[:, :], slow_keys))
                        dve.nop(nofuse=True)
                        rs.done(V.match_replace(slow_keys, top8[:, :], slow_keys, 0.0))
                        rstep(V.tensor_scalar(inv8[:, :], top8[:, :], 0.5, None, ALU.is_lt))
                        rs.done(V.tensor_scalar(pen8[:, :], inv8[:, :], NEG, None, ALU.mult))
                        rstep(V.scalar_tensor_tensor(idxf8[:, :], inv8[:, :], float(N + 1), top8[:, :], ALU.mult,
                                                     ALU.add))
                        V.tensor_scalar(idx8[:, :], idxf8[:, :], -1.0, None, ALU.add).then_inc(round_lists, 1)
                        dve.wait_ge(round_gathered, n * 128 + 128)
                        L = lg8[:, 0:8, :]
                        rstep(V.tensor_tensor(L, G[:, 0, 0:8, D:ROW], e_l.broadcast_to([P, 8, HEADS]), ALU.add))
                        rstep(V.scalar_tensor_tensor(L, L, 0.2, L, ALU.mult, ALU.max))
                        rstep(V.tensor_tensor(L, L, along(pen8[:, :], HEADS), ALU.add))
                        rstep(V.tensor_reduce(rmax8[:, :], L.rearrange("p k h -> p h k"), AX, ALU.max))
                        rs.done(V.tensor_tensor(newmax[:, :], oldmax[:, :], rmax8[:, :], ALU.max))
                        rstep(V.tensor_copy(lg8[:, 8, :], oldmax[:, :]))
                        V.tensor_tensor(lg8[:, :, :], lg8[:, :, :],
                                        newmax[:, :].unsqueeze(1).broadcast_to([P, 9, HEADS]),
                                        ALU.subtract).then_inc(round_logits, 1)
                        rs.done(V.tensor_copy(oldmax[:, :], newmax[:, :]))
                        dve.wait_ge(round_probs, n + 1)
                        rs.done(V.tensor_reduce(sum8[:, :], prob8[:, 0:8, :].rearrange("p k h -> p h k"), AX,
                                                ALU.add))
                        rstep(V.tensor_tensor(den8[:, :], den8[:, :], prob8[:, 8, :], ALU.mult))
                        rs.done(V.tensor_tensor(den8[:, :], den8[:, :], sum8[:, :], ALU.add))
                        rows = G[:, 0, 0:8, 0:D].rearrange("p k (h d) -> p k h d", h=HEADS)
                        rstep(V.tensor_tensor(rows, rows, prob8[:, 0:8, :].unsqueeze(3)
                                              .broadcast_to([P, 8, HEADS, HD]), ALU.mult))
                        rs.done(V.tensor_reduce(part[:, :], G[:, 0, 0:8, 0:D].rearrange("p k d -> p d k"), AX,
                                                ALU.add))
                        av = acc[:, :].rearrange(heads, h=HEADS)
                        rstep(V.tensor_tensor(av, av, along(prob8[:, 8, :], HD), ALU.mult))
                        rstep(V.tensor_tensor(acc[:, :], acc[:, :], part[:, :], ALU.add))
                        assert rs.n == ROUND, rs.n
                step(V.reciprocal(den8[:, :], den8[:, :]))
                step(V.tensor_tensor(o[:, 0, :].rearrange(heads, h=HEADS), acc[:, :].rearrange(heads, h=HEADS),
                                     along(den8[:, :], HD), ALU.mult))
                V.tensor_tensor(o[:, 0, :], o[:, 0, :], biasb[:, :], ALU.add).then_inc(slow_o, 1)
                assert sl.n == SLOW, sl.n
                dve.wait_ge(slow_expo, rank + 1)
                tail = Steps(dve, flags_step, rank * 4 + 3, apart=True)

                def tstep(ins):
                    tail.done(ins)
                    tail.wait()

                tstep(V.tensor_scalar(eo[:, 0, :], eo[:, 0, :], 1.0, None, ALU.add))
                tstep(V.reciprocal(eo[:, 0, :], eo[:, 0, :]))
                z = H[:, bass.ds(t, 1), 0:D]
                tstep(V.tensor_tensor(z, o[:, 0:1, :], eo[:, 0:1, :], ALU.mult))
                tstep(V.tensor_tensor(sq[:, 0:1, :], z, z, ALU.mult))
                V.tensor_reduce(nrm[:, bass.ds(t, 1)], sq[:, 0:1, :], AX, ALU.add).then_inc(slow_free, 1)

            with dve.If(any_flagged(dve) > 0):
                fl.done(V.memset(tally[:, :, :], 0.0))
                fl.wait()
                V.drain().then_inc(slow_free, 1)
                dve.wait_ge(colid_landed, 16)
                with dve.Fori(0, T) as t:
                    tl = Steps(dve, tally_step, t * 3, apart=True)
                    tl.done(V.tensor_tensor(tally[0:1, bass.ds(t + 1, 1), 0], tally[0:1, bass.ds(t, 1), 0],
                                            flagrow[0:1, bass.ds(t, 1)], ALU.add))
                    tl.done(V.tensor_copy(tally[0:1, bass.ds(t + 1, 1), 1], tally[0:1, bass.ds(t, 1), 1]))
                    tl.done(V.tensor_copy(ctl[0:1, bass.ds(t, 1), 0], flagrow[0:1, bass.ds(t, 1)]))
                    tl.wait()
                    V.tensor_copy(ctl[0:1, bass.ds(t, 1), 1:3], tally[0:1, bass.ds(t, 1), :]).then_inc(ctl_ready, 1)
                    flag, rank, base = control(dve, t)
                    with dve.If(flag > 0):
                        slow_tile(t, rank, base)
            V.drain().then_inc(slow_done, 1)
            dve.wait_ge(slow_done, 1)

            fin = Steps(dve, fin_step)

            def fstep(ins):
                fin.done(ins)
                fin.wait()

            dve.wait_ge(norms_rooted, 1)
            V.tensor_scalar(sm[:, 1, :], sm[:, 0, :], EPS_NORM, None, ALU.max).then_inc(norms_kept, 1)
            dve.wait_ge(norms_kept, 1)
            fstep(V.reciprocal(sm[:, 3, :], sm[:, 1, :]))
            dve.wait_ge(tanh_ready, 1)
            fstep(V.tensor_tensor(sm[:, 4, :], sm[:, 2, :], sm[:, 3, :], ALU.mult))
            for i in range(NPIECE):
                here = slice(i * PIECE, (i + 1) * PIECE)
                fstep(V.tensor_tensor(H[:, here, 0:D], H[:, here, 0:D], along(sm[:, 4, here], D), ALU.mult))
                V.tensor_tensor(X[:, here, :], X[:, here, :], H[:, here, 0:D], ALU.add).then_inc(out_ready, 1)


def kernel(x, adj, L0_gnn_W, L0_gnn_a_l, L0_gnn_a_r, L0_gnn_bias):
    import numpy as np
    import ml_dtypes
    import concourse.bacc as bacc
    from concourse.bass_utils import run_bass_kernel_spmd

    N = 8192
    W = N // BITS
    pos = np.arange(W)
    packw = np.zeros((P, BITS, P), np.float32)
    packw[np.arange(P), :, np.arange(P)] = 2.0 ** (np.arange(BITS) - 1)
    consts = {
        "ident": np.eye(P, dtype=np.float32),
        "packw": packw.astype(ml_dtypes.bfloat16),
        "posrow": np.stack([np.full(W, (2 ** BITS - 1) / 2), (pos // 32 * 32) / W, (pos % 32) / W]).astype(ml_dtypes.bfloat16),
        "onesrow": np.ones((3, P), ml_dtypes.bfloat16),
        "selfid": (np.arange(P)[:, None] + P * np.arange(N // P)[None, :] + 1).astype(np.float32),
        "headsel": (np.arange(P)[:, None] // (P // HEADS) == np.arange(HEADS)[None, :]).astype(np.float32),
        "colid": np.arange(1, N + 1, dtype=np.float32)[None, :],
    }
    nc = bacc.Bacc("TRN2", target_bir_lowering=False, num_devices=1)
    arrays = {"x": x, "adj": adj, "W": L0_gnn_W, "a_l": L0_gnn_a_l, "a_r": L0_gnn_a_r, "bias": L0_gnn_bias, **consts}
    args, feed = [], {}
    for name, a in arrays.items():
        a = np.ascontiguousarray(a)
        feed[f"in_{name}"] = a
        args.append(nc.dram_tensor(f"in_{name}", a.shape, mybir.dt.from_np(a.dtype), kind="ExternalInput").ap())
    args.append(nc.dram_tensor("out", (N, P), F32, kind="ExternalOutput").ap())
    build(nc, *args)
    r = run_bass_kernel_spmd(nc, [feed], core_ids=[0])
    return r.results[0]["out"]
```

```python
from contextlib import ExitStack

import concourse.bass as bass
from concourse import mybir

P = 128
ALU = mybir.AluOpType
ACT = mybir.ActivationFunctionType
AX = mybir.AxisListType.X
F32 = mybir.dt.float32
BF16 = mybir.dt.bfloat16
I32 = mybir.dt.int32
U32 = mybir.dt.uint32

HEADS = 4
BITS = 8
SEG = 64
SLOTS = 24
NEAR = 12
OCT = 8
ROUNDS = SLOTS // 8
PEEL = 3
CHUNK = 2048
MAX_TANH_ARG = 1.0 - 1e-05
EPS_LN = 1e-05
EPS_NORM = 1e-15
NEG = -1e30


class Steps:

    def __init__(self, eng, sem, base=0, apart=False):
        self.eng, self.sem, self.base, self.n, self.apart = eng, sem, base, 0, apart

    def done(self, ins):
        self.n += 1
        ins.then_inc(self.sem, 1)

    def wait(self):
        self.eng.wait_ge(self.sem, self.base + self.n)
        if self.apart:
            self.eng.nop(nofuse=True)


def build(nc, x, adj, W, a_l, a_r, bias, ident_d, packw_d, posrow_d, onesrow_d, selfid_d, headsel_d, colid_d, ltri_d, allones_d, iota_e_d, out):
    N, D = x.shape
    T = N // P
    PAIRS = T // 2
    WORDS = N // BITS
    NCH = N // CHUNK
    BPC = CHUNK // WORDS
    NSEG = WORDS // SEG
    CANDS = NSEG * 8
    HD = D // HEADS
    ROW = D + HEADS
    RW = ROW + HEADS
    PIECE = 16
    NPIECE = T // PIECE
    QUADS = T // 4
    EXPO = 127 * WORDS
    ENTRIES = PEEL * SLOTS
    N_EXT, N_DEC, N_ATT, N_VL, N_VATT, N_MERGE = 2 * ROUNDS, 39, 6, 9, 6, 11
    N_POL = 10
    POLISH = (0, 1, 2, 3)
    POLISH_ACT = (0, 2, 3, 4)
    EARLY = (1, 3)
    VAT = 6
    OVER = SLOTS - NEAR
    FREE = 2

    table = nc.dram_tensor("table", (N, ROW), F32, kind="Internal").ap()

    with ExitStack() as ctx:
        def sb(name, shape, dt=F32):
            return ctx.enter_context(nc.sbuf_tensor(name, shape, dt))

        def ps(name, shape, dt=F32):
            return ctx.enter_context(nc.psum_tensor(name, shape, dt))

        def sem(name):
            return ctx.enter_context(nc.semaphore(name))

        ident = sb("ident", [P, P])
        packw = sb("packw", [P, BITS, P], BF16)
        posrow = sb("posrow", [3, WORDS], BF16)
        onesrow = sb("onesrow", [3, P], BF16)
        selfid = sb("selfid", [P, T])
        headsel = sb("headsel", [P, HEADS])
        biasb = sb("biasb", [P, D])
        neg_tiny = sb("neg_tiny", [P, 1])
        wraw = sb("wraw", [P, D])
        acol = sb("acol", [P, 2])
        ablk = sb("ablk", [P, 2 * HEADS])
        waug = sb("waug", [P, RW])
        X = sb("X", [P, T, D])
        H = sb("H", [P, T, RW])
        adjbuf = sb("adjbuf", [P, 2, NCH, CHUNK])
        signs = sb("signs", [P, NCH, CHUNK], BF16)
        GG = sb("GG", [P, 2 * NEAR + OVER, ROW])
        G = GG[:, 0:2 * NEAR, :].rearrange("p (b k) r -> p b k r", b=2)
        GV = GG[:, 2 * NEAR:, :]
        mean = sb("mean", [P, T])
        stat = sb("stat", [P, 2, T])
        root = sb("root", [P, 2, T])
        sm = sb("sm", [P, 8, T])
        rT = sb("rT", [P, 2, 512])
        cand = sb("cand", [P, CANDS])
        cand2 = sb("cand2", [P, CANDS])
        words = sb("words", [P, 2, SLOTS])
        keyi = sb("keyi", [P, 2, SLOTS], I32)
        posi = sb("posi", [P, 2, SLOTS], I32)
        wi = sb("wi", [P, 2, SLOTS], I32)
        wf = sb("wf", [P, 2, SLOTS])
        topbit = sb("topbit", [P, 2, SLOTS], I32)
        bitno = sb("bitno", [P, 2, SLOTS], I32)
        ents = sb("ents", [P, 2, ENTRIES])
        notself = sb("notself", [P, 2, ENTRIES])
        ents2 = sb("ents2", [P, 2, ENTRIES])
        top = sb("top", [P, 2, SLOTS])
        topc = sb("topc", [P, 2, SLOTS])
        inv = sb("inv", [P, 2, SLOTS])
        idxf = sb("idxf", [P, 2, SLOTS])
        idx = sb("idx", [P, 2, 2, SLOTS], U32)
        pen = sb("pen", [P, 2, 2, SLOTS])
        over4 = sb("over4", [P, 2, 4])
        over = sb("over", [P, T])
        lg = sb("lg", [P, 2, NEAR + 1, HEADS])
        prob = sb("prob", [P, 2, NEAR + 1, HEADS])
        rowmax = sb("rowmax", [P, OCT, HEADS])
        den = sb("den", [P, OCT, HEADS])
        kept_o = sb("kept_o", [P, 2, OCT, D])
        kept = kept_o[:, 0, :, :]
        o = kept_o[:, 1, :, :]
        ltri = sb("ltri", [P, P], BF16)
        allones = sb("allones", [P, P], BF16)
        iota_e = sb("iota_e", [P, P])
        zeros = sb("zeros", [P, OCT], BF16)
        more = sb("more", [P, OCT], BF16)
        moref = sb("moref", [P, OCT])
        nomore = sb("nomore", [P, OCT])
        dest = sb("dest", [P, OCT])
        lost = sb("lost", [P, OCT])
        far = sb("far", [P, OCT, OVER + HEADS])
        place = sb("place", [P, OCT, P])
        placeT = rT[:, :, :].rearrange("p b n -> p (b n)").rearrange("p (t e) -> p t e", e=P)
        vfar = sb("vfar", [P, OVER + HEADS])
        vinv = sb("vinv", [P, OVER])
        vidxf = sb("vidxf", [P, OVER])
        vidx = sb("vidx", [P, OVER], U32)
        vpen = sb("vpen", [P, OVER])
        vlg = sb("vlg", [P, OVER, HEADS])
        vprob = sb("vprob", [P, OVER, HEADS])
        vres = sb("vres", [P, D + 2 * HEADS])
        m12 = sb("m12", [P, 2, OCT, HEADS])
        c12 = sb("c12", [P, 2, OCT, HEADS])
        allmax = sb("allmax", [P, OCT, HEADS])
        allden = sb("allden", [P, OCT, HEADS])
        selfp = sb("selfp", [P, 2, D])
        eo = place
        nrm = sb("nrm", [P, OCT])
        root8 = sb("root8", [P, OCT])
        norm8 = sb("norm8", [P, OCT])
        tanh8 = sb("tanh8", [P, OCT])
        scale8 = sb("scale8", [P, OCT])

        ones = sb("ones", [P, 1])
        rowflag = sb("rowflag", [P, T])
        flagrow = sb("flagrow", [1, T])
        anyflag = sb("anyflag", [1, 1])
        anyi = sb("anyi", [1, 1], I32)
        tally = sb("tally", [1, T + 1, 2])
        ctl = sb("ctl", [1, T, 3], I32)
        degree = sb("degree", [P, 1])
        maxdeg = sb("maxdeg", [1, 1])
        degi = sb("degi", [1, 1], I32)
        rounds = sb("rounds", [1, T], I32)
        top8 = sb("top8", [P, 8])
        topc8 = sb("topc8", [P, 8])
        inv8 = sb("inv8", [P, 8])
        idxf8 = sb("idxf8", [P, 8])
        idx8 = sb("idx8", [P, 8], U32)
        pen8 = sb("pen8", [P, 8])
        lg8 = sb("lg8", [P, 9, HEADS])
        prob8 = sb("prob8", [P, 9, HEADS])
        newmax = sb("newmax", [P, HEADS])
        oldmax = sb("oldmax", [P, HEADS])
        rmax8 = sb("rmax8", [P, HEADS])
        den8 = sb("den8", [P, HEADS])
        sum8 = sb("sum8", [P, HEADS])
        acc = sb("acc", [P, D])
        part = sb("part", [P, D])

        keys = ps("keys", [P, 2, WORDS])
        po = ps("po", [P, 2, 512])
        pt = ps("pt", [P, 2, 512])

        x_landed = [sem(f"x_landed{i}") for i in range(NPIECE)]
        w_landed = sem("w_landed")
        const_landed = sem("const_landed")
        adj_landed = [sem(f"adj_landed{i}") for i in range(2 * NCH)]
        cleared = sem("cleared")
        tiny_set = sem("tiny_set")
        w_turned = sem("w_turned")
        a_spread = sem("a_spread")
        waug_ready = sem("waug_ready")
        centred = sem("centred")
        squared = sem("squared")
        relu_ready = sem("relu_ready")
        sq_read = sem("sq_read")
        turned = sem("turned")
        rT_ready = sem("rT_ready")
        h_done = sem("h_done")
        h_read = sem("h_read")
        prep_step = sem("prep_step")
        stat_ready = sem("stat_ready")
        root_ready = sem("root_ready")
        arg_ready = sem("arg_ready")
        logs_ready = sem("logs_ready")
        scaled = sem("scaled")
        table_stored = sem("table_stored")
        signed = sem("signed")
        packed = sem("packed")
        keys_read = sem("keys_read")
        ext_step = sem("ext_step")
        dec_step = sem("dec_step")
        lists_ready = sem("lists_ready")
        gathered = [sem("gathered0"), sem("gathered1")]
        att_step = sem("att_step")
        logits_ready = sem("logits_ready")
        probs_ready = sem("probs_ready")
        weighted = sem("weighted")
        summed = sem("summed")
        sums_kept = sem("sums_kept")
        more_made = sem("more_made")
        ranked = sem("ranked")
        vl_step = sem("vl_step")
        placed = sem("placed")
        far_moved = sem("far_moved")
        place_turned = sem("place_turned")
        placeT_ready = sem("placeT_ready")
        vlists_ready = sem("vlists_ready")
        vgathered = sem("vgathered")
        vatt_step = sem("vatt_step")
        vlogits_ready = sem("vlogits_ready")
        vprobs_ready = sem("vprobs_ready")
        vweighted = sem("vweighted")
        vsummed = sem("vsummed")
        vres_ready = sem("vres_ready")
        sent_back = sem("sent_back")
        merge_step = sem("merge_step")
        pol_step = sem("pol_step")
        maxima_ready = sem("maxima_ready")
        scales_ready = sem("scales_ready")
        merged = sem("merged")
        o_ready = sem("o_ready")
        expo_ready = sem("expo_ready")
        norms_ready = sem("norms_ready")
        norms_rooted = sem("norms_rooted")
        norms_kept = sem("norms_kept")
        tanh_ready = sem("tanh_ready")
        flags_step = sem("flags_step")
        flags_counted = sem("flags_counted")
        any_ready = sem("any_ready")
        ctl_ready = sem("ctl_ready")
        colid_landed = sem("colid_landed")
        slow_free = sem("slow_free")
        slow_adj = sem("slow_adj")
        slow_step = sem("slow_step")
        degrees_ready = sem("degrees_ready")
        degrees_turned = sem("degrees_turned")
        rounds_ready = sem("rounds_ready")
        round_step = sem("round_step")
        round_lists = sem("round_lists")
        round_gathered = sem("round_gathered")
        round_logits = sem("round_logits")
        round_probs = sem("round_probs")
        slow_o = sem("slow_o")
        slow_expo = sem("slow_expo")
        main_done = sem("main_done")
        tally_step = sem("tally_step")
        tail_step = sem("tail_step")
        slow_nrm = sem("slow_nrm")
        slow_root = sem("slow_root")
        slow_norm = sem("slow_norm")
        slow_tanh = sem("slow_tanh")
        slow_out_ready = sem("slow_out_ready")
        slow_stored = sem("slow_stored")
        out_ready = sem("out_ready")
        out_stored = sem("out_stored")

        SPAN = PIECE * D
        GGflat = GG[:, :, :].rearrange("p k r -> p (k r)")
        halves = (kept_o[:, :, :, :].rearrange("p a t c -> p (a t c)"), GGflat)

        def centred_piece(b):
            return halves[b][:, 0:SPAN].rearrange("p (t c) -> p t c", c=D)

        squares = GGflat[:, SPAN:2 * SPAN].rearrange("p (t c) -> p t c", c=D)
        x_t = x.rearrange("(t p) c -> p t c", p=P)
        out_t = out.rearrange("(t p) c -> p t c", p=P)
        table_t = table.rearrange("(t p) c -> p t c", p=P)

        def along(ap, n):
            return ap.unsqueeze(2).broadcast_to([ap.shape[0], ap.shape[1], n])

        colid = adjbuf[:, 1, :, :].rearrange("p c n -> p (c n)")
        slow_keys = adjbuf[:, 0, :, :].rearrange("p c n -> p (c n)")
        slow_own = G[:, 1, 0, :]
        slow_x, slow_out = kept[:, 0, :], kept[:, 1, :]
        MAXROUNDS = N // 8

        def any_flagged(eng):
            eng.wait_ge(any_ready, 1)
            eng.nop(nofuse=True)
            return eng.value_load(anyi[0:1, 0:1], min_val=0, max_val=T)

        def control(eng, t):
            eng.wait_ge(ctl_ready, t + 1)
            eng.nop(nofuse=True)
            flag = eng.value_load(ctl[0:1, bass.ds(t, 1), 0], min_val=0, max_val=1)
            rank = eng.value_load(ctl[0:1, bass.ds(t, 1), 1], min_val=0, max_val=T)
            base = eng.value_load(ctl[0:1, bass.ds(t, 1), 2], min_val=0, max_val=T * MAXROUNDS)
            return flag, rank, base

        def round_count(eng, t, rank):
            eng.wait_ge(rounds_ready, rank + 1)
            eng.nop(nofuse=True)
            return eng.value_load(rounds[0:1, bass.ds(t, 1)], min_val=0, max_val=MAXROUNDS)

        def round_loop(eng, count):
            with eng.Fori(0, MAXROUNDS, 32) as r0:
                with eng.If(r0 < count):
                    with eng.Fori(0, 32) as r1:
                        yield r0 + r1

        block = ctx.enter_context(nc.Block())

        @block.sync
        def _(sp):
            def load_adj(t, b, c):
                sp.dma_start(adjbuf[:, b, c, :], adj[bass.ds(t * P, P), c * CHUNK:(c + 1) * CHUNK]) \
                    .then_inc(adj_landed[b * NCH + c], 16)

            for i in range(NPIECE):
                sp.dma_start(X[:, i * PIECE:(i + 1) * PIECE, :], x_t[:, i * PIECE:(i + 1) * PIECE, :]) \
                    .then_inc(x_landed[i], 16)
                if i == 0:
                    for dst, src in ((wraw[:, :], W), (acol[:, 0:1], a_r.rearrange("h (d u) -> (h d) u", u=1)),
                                     (acol[:, 1:2], a_l.rearrange("h (d u) -> (h d) u", u=1)),
                                     (ident[:, :], ident_d), (headsel[:, :], headsel_d)):
                        sp.dma_start(dst, src).then_inc(w_landed, 16)
            for dst, src in ((packw[:, :, :], packw_d), (posrow[:, :], posrow_d), (onesrow[:, :], onesrow_d),
                             (selfid[:, :], selfid_d), (ltri[:, :], ltri_d), (allones[:, :], allones_d),
                             (iota_e[:, :], iota_e_d),
                             (biasb[:, :], bias.unsqueeze(0).broadcast_to([P, D]))):
                sp.dma_start(dst, src).then_inc(const_landed, 16)
            for t in range(2):
                for c in range(NCH):
                    load_adj(t, t, c)
            for i in range(NPIECE):
                sp.wait_ge(scaled, i + 1)
                sp.dma_start(table_t[:, i * PIECE:(i + 1) * PIECE, :], H[:, i * PIECE:(i + 1) * PIECE, 0:ROW]) \
                    .then_inc(table_stored, 16)
            with sp.Fori(1, PAIRS) as pair:
                for b in range(2):
                    for c in range(NCH):
                        sp.wait_ge(signed, pair * (2 * NCH) + (b * NCH + c + 1 - 2 * NCH))
                        load_adj(pair * 2 + b, b, c)
            with sp.If(any_flagged(sp) > 0):
                sp.dma_start(colid, colid_d.broadcast_to([P, N])).then_inc(colid_landed, 16)
                with sp.Fori(0, T) as t:
                    flag, rank, _ = control(sp, t)
                    with sp.If(flag > 0):
                        sp.wait_ge(slow_free, rank + 1)
                        sp.dma_start(slow_keys, adj[bass.ds(t * P, P), :]).then_inc(slow_adj, 16)
                        sp.dma_start(slow_own, table[bass.ds(t * P, P), :]).then_inc(slow_adj, 16)
                        sp.dma_start(slow_x, x[bass.ds(t * P, P), :]).then_inc(slow_adj, 16)
                        sp.wait_ge(out_stored, 16 * (T // OCT))
                        sp.wait_ge(slow_out_ready, rank + 1)
                        sp.dma_start(out[bass.ds(t * P, P), :], slow_out).then_inc(slow_stored, 16)
                        sp.wait_ge(slow_stored, rank * 16 + 16)
                        sp.nop(nofuse=True)
            sp.wait_ge(out_stored, 16 * (T // OCT))

        @block.gpsimd
        def _(pool):
            nc.gpsimd.memset(GGflat[:, :], 0.0).then_inc(cleared, 1)
            pool.wait_ge(table_stored, 16 * NPIECE)

            def fetch(buf, index, done):
                for k in range(NEAR):
                    nc.gpsimd.indirect_dma_start(
                        buf[:, k, :], None, table, bass.IndirectOffsetOnAxis(ap=index[:, k:k + 1], axis=0),
                        bounds_check=N - 1, oob_is_err=False).then_inc(done, 16)

            with pool.Fori(0, T // OCT) as g:
                for i in range(OCT // 2):
                    if 2 * i == VAT:
                        pool.wait_ge(vlists_ready, g + 1)
                        pool.nop(nofuse=True)
                        fetch(GV[:, :, :], vidx[:, :], vgathered)
                    pool.wait_ge(lists_ready, g * (OCT // 2) + (i + 1))
                    for b in range(2):
                        pool.wait_ge(summed, g * OCT + (2 * i + b - 1 + FREE))
                        pool.nop(nofuse=True)
                        fetch(G[:, b, :, :], idx[:, i % 2, b, :], gathered[b])

            with pool.If(any_flagged(pool) > 0):
                with pool.Fori(0, T) as t:
                    flag, rank, base = control(pool, t)
                    with pool.If(flag > 0):
                        count = round_count(pool, t, rank)
                        for r in round_loop(pool, count):
                            with pool.If(r < count):
                                pool.wait_ge(round_lists, base + r + 1)
                                pool.nop(nofuse=True)
                                for k in range(8):
                                    nc.gpsimd.indirect_dma_start(
                                        G[:, 0, k, :], None, table,
                                        bass.IndirectOffsetOnAxis(ap=idx8[:, k:k + 1], axis=0),
                                        bounds_check=N - 1, oob_is_err=False).then_inc(round_gathered, 16)

        @block.scalar
        def _(act):
            def sign(t, b, first=False):
                for c in range(NCH):
                    act.wait_ge(adj_landed[b * NCH + c], (t - b) * 8 + 16)
                    if not first:
                        act.wait_ge(packed, t * NCH + (c + 1 - NCH))
                    nc.scalar.activation(signs[:, c, :], adjbuf[:, b, c, :], ACT.Sign, bias=neg_tiny[:, :]) \
                        .then_inc(signed, 1)

            def keep(quad):
                act.wait_ge(h_done, quad + 1)
                for j in range(2):
                    last = nc.scalar.copy(H[:, 4 * quad + 2 * j:4 * quad + 2 * j + 2, :],
                                          po[:, j, 0:2 * RW].rearrange("p (t c) -> p t c", c=RW))
                last.then_inc(h_read, 1)

            act.wait_ge(tiny_set, 1)
            for i in range(NPIECE):
                act.wait_ge(centred, i + 1)
                if i:
                    act.wait_ge(sq_read, 2 * i)
                else:
                    act.wait_ge(cleared, 1)
                nc.scalar.activation(squares, centred_piece(i % 2), ACT.Square).then_inc(squared, 1)
                act.wait_ge(relu_ready, i + 1)
                act.wait_ge(sq_read, 2 * i + 1)
                nc.scalar.activation(squares, centred_piece(i % 2), ACT.Square).then_inc(squared, 1)
                for j in range(PIECE // 4):
                    quad = i * (PIECE // 4) + j
                    act.wait_ge(turned, quad + 1)
                    if quad >= 2:
                        act.wait_ge(h_done, quad - 1)
                    nc.scalar.copy(rT[:, quad % 2, :], pt[:, quad % 2, :]).then_inc(rT_ready, 1)
                    if quad:
                        keep(quad - 1)
                if i in EARLY:
                    sign(EARLY.index(i), EARLY.index(i), i == EARLY[0])
            keep(QUADS - 1)
            act.wait_ge(stat_ready, 1)
            nc.scalar.activation(root[:, :, :], stat[:, :, :], ACT.Sqrt).then_inc(root_ready, 1)
            act.wait_ge(arg_ready, 1)
            nc.scalar.activation(sm[:, 2, :], sm[:, 1, :], ACT.Ln, bias=1.0, scale=1.0).then_inc(logs_ready, 1)
            nc.scalar.activation(sm[:, 3, :], sm[:, 1, :], ACT.Ln, bias=1.0, scale=-1.0).then_inc(logs_ready, 1)

            def keep_sums(g, j):
                if j == 0:
                    act.wait_ge(merged, g + 1)
                act.wait_ge(summed, g * OCT + (j + 1 + FREE))
                nc.scalar.copy(kept[:, j, :], po[:, j % 2, 0:D]).then_inc(sums_kept, 1)

            def polish(g, part):
                if part == 0:
                    act.wait_ge(o_ready, g)
                    nc.scalar.activation(eo[:, :, :], o[:, :, :], ACT.Exp, scale=-1.0).then_inc(expo_ready, 1)
                elif part == 1:
                    act.wait_ge(norms_ready, g)
                    nc.scalar.activation(root8[:, :], nrm[:, :], ACT.Sqrt).then_inc(norms_rooted, 1)
                elif part == 2:
                    act.wait_ge(norms_kept, g)
                    nc.scalar.activation(tanh8[:, :], norm8[:, :], ACT.Tanh).then_inc(tanh_ready, 1)
                else:
                    act.wait_ge(out_ready, g)
                    act.dma_start(out_t[:, bass.ds((g - 1) * OCT, OCT), :], X[:, bass.ds((g - 1) * OCT, OCT), :]) \
                        .then_inc(out_stored, 16)

            def octet(g, first, last):
                for j in range(OCT):
                    t = g * OCT + j
                    act.wait_ge(logits_ready, t + 1)
                    nc.scalar.activation(prob[:, j % 2, :, :], lg[:, j % 2, :, :], ACT.Exp).then_inc(probs_ready, 1)
                    if not first and j in POLISH_ACT:
                        polish(g, POLISH_ACT.index(j))
                    if j:
                        keep_sums(g, j - 1)
                    if j == VAT:
                        act.wait_ge(vlogits_ready, g + 1)
                        nc.scalar.activation(vprob[:, :, :], vlg[:, :, :], ACT.Exp).then_inc(vprobs_ready, 1)
                    if not last or j + 5 < OCT:
                        sign(t + 5, (j + 1) % 2)
                    if j == 3:
                        for h in range(2):
                            act.wait_ge(place_turned, g * 2 + (h + 1))
                            nc.scalar.copy(placeT[:, 4 * h:4 * h + 4, :].rearrange("p t e -> p (t e)"),
                                           pt[:, 0, :]).then_inc(placeT_ready, 1)
                keep_sums(g, OCT - 1)
                act.wait_ge(maxima_ready, g + 1)
                nc.scalar.activation(c12[:, :, :, :], m12[:, :, :, :], ACT.Exp).then_inc(scales_ready, 1)

            act.nop(nofuse=True).then_inc(sums_kept, FREE)
            for t in range(len(EARLY), 5):
                sign(t, t % 2)
            octet(0, True, False)
            with act.Fori(1, T // OCT - 1) as g:
                octet(g, False, False)
            octet(T // OCT - 1, False, True)
            for n in range(len(POLISH)):
                polish(T // OCT, n)
            with act.If(any_flagged(act) > 0):
                with act.Fori(0, T) as t:
                    flag, rank, base = control(act, t)
                    with act.If(flag > 0):
                        count = round_count(act, t, rank)
                        for r in round_loop(act, count):
                            with act.If(r < count):
                                act.wait_ge(round_logits, base + r + 1)
                                nc.scalar.activation(prob8[:, :, :], lg8[:, :, :], ACT.Exp).then_inc(round_probs, 1)
                        act.wait_ge(slow_o, rank + 1)
                        nc.scalar.activation(eo[:, 0, :], o[:, 0, :], ACT.Exp, scale=-1.0).then_inc(slow_expo, 1)
                        act.wait_ge(slow_nrm, rank + 1)
                        nc.scalar.activation(root8[:, 0:1], nrm[:, 0:1], ACT.Sqrt).then_inc(slow_root, 1)
                        act.wait_ge(slow_norm, rank + 1)
                        nc.scalar.activation(tanh8[:, 0:1], norm8[:, 0:1], ACT.Tanh).then_inc(slow_tanh, 1)

        @block.tensor
        def _(pe):
            pe.wait_ge(w_landed, 16 * 5)
            nc.tensor.transpose(pt[:, 0, 0:P], wraw[:, :], ident[:, :]).then_inc(w_turned, 1)
            pe.wait_ge(a_spread, 1)
            nc.tensor.matmul(pt[:, 1, 0:2 * HEADS], wraw[:, :], ablk[:, :], start=True, stop=True) \
                .then_inc(w_turned, 1)
            pe.wait_ge(waug_ready, 1)

            def turn(quad, b, first):
                pe.wait_ge(relu_ready, quad // (PIECE // 4) + 1)
                if not first:
                    pe.wait_ge(rT_ready, quad - 1)
                for j in range(4):
                    tt = (quad % (PIECE // 4)) * 4 + j
                    last = nc.tensor.transpose(pt[:, b, j * P:(j + 1) * P],
                                               centred_piece(quad // (PIECE // 4) % 2)[:, tt, :], ident[:, :])
                last.then_inc(turned, 1)

            def project(quad, b):
                pe.wait_ge(rT_ready, quad + 1)
                if quad:
                    pe.wait_ge(h_read, quad)
                for j in range(4):
                    last = nc.tensor.matmul(po[:, j // 2, (j % 2) * RW:(j % 2 + 1) * RW],
                                            rT[:, b, j * P:(j + 1) * P], waug[:, :], start=True, stop=True)
                last.then_inc(h_done, 1)

            def pack(t, b):
                if not isinstance(t, int) or t >= 2:
                    pe.wait_ge(keys_read, t - 1)
                for half in range(WORDS // 512):
                    nc.tensor.matmul(keys[:, b, half * 512:(half + 1) * 512], onesrow[:, :],
                                     posrow[:, half * 512:(half + 1) * 512], start=True, stop=False)
                for c in range(NCH):
                    pe.wait_ge(signed, t * NCH + (c + 1))
                    for k in range(BPC):
                        for half in range(WORDS // 512):
                            at = k * WORDS + half * 512
                            last = nc.tensor.matmul(keys[:, b, half * 512:(half + 1) * 512],
                                                    packw[:, c * BPC + k, :], signs[:, c, at:at + 512],
                                                    start=False, stop=(c * BPC + k == BITS - 1))
                    last.then_inc(packed, 1)

            turn(0, 0, True)
            for quad in range(QUADS):
                if quad + 1 < QUADS:
                    turn(quad + 1, (quad + 1) % 2, quad + 1 < 2)
                project(quad, quad % 2)
                if (quad + 1) % (PIECE // 4) == 0 and quad // (PIECE // 4) in EARLY:
                    if quad // (PIECE // 4) == EARLY[0]:
                        pe.wait_ge(const_landed, 16 * 8)
                    pack(EARLY.index(quad // (PIECE // 4)), EARLY.index(quad // (PIECE // 4)))
            pe.wait_ge(h_read, QUADS)

            def sums(t, b):
                pe.wait_ge(sums_kept, t + (FREE - 1))
                pe.wait_ge(weighted, t + 1)
                for k in range(NEAR):
                    nc.tensor.matmul(po[:, b, 0:D], ident[:, :], G[:, b, k, 0:D], start=(k == 0), stop=False)
                nc.tensor.matmul(po[:, b, 0:D], ident[:, :], selfp[:, b, :], start=False, stop=True) \
                    .then_inc(summed, 1)

            def overflow_lists(g):
                pe.wait_ge(merged, g + 1)
                pe.wait_ge(more_made, g * (OCT // 2) + OCT // 2)
                nc.tensor.matmul(pt[:, 1, 0:OCT], ltri[:, :], more[:, :], start=True, stop=False)
                for j in range(OCT - 1):
                    nc.tensor.matmul(pt[:, 1, j + 1:OCT], allones[:, :],
                                     more[:, j:j + 1].broadcast_to([P, OCT - 1 - j]), start=False, stop=False)
                nc.tensor.matmul(pt[:, 1, 0:OCT], allones[:, :], zeros[:, :], start=False, stop=True) \
                    .then_inc(ranked, 1)
                pe.wait_ge(placed, g + 1)
                for j in range(OCT):
                    last = nc.tensor.matmul(pt[:, 1, 16:16 + OVER + HEADS], place[:, j, :], far[:, j, :],
                                            start=(j == 0), stop=(j == OCT - 1))
                last.then_inc(far_moved, 1)
                for h in range(2):
                    if h:
                        pe.wait_ge(placeT_ready, g * 2 + 1)
                    for j in range(4):
                        last = nc.tensor.transpose(pt[:, 0, j * P:(j + 1) * P], place[:, 4 * h + j, :], ident[:, :])
                    last.then_inc(place_turned, 1)

            def overflow_sums(g):
                pe.wait_ge(placeT_ready, g * 2 + 2)
                pe.wait_ge(vweighted, g + 1)
                for k in range(OVER):
                    last = nc.tensor.matmul(pt[:, 0, 0:D], ident[:, :], GV[:, k, 0:D], start=(k == 0),
                                            stop=(k == OVER - 1))
                last.then_inc(vsummed, 1)

            def send_back(g):
                pe.wait_ge(vres_ready, g + 1)
                pe.wait_ge(sums_kept, g * OCT + (OCT + FREE))
                for j in range(OCT):
                    nc.tensor.matmul(po[:, 0, j * 2 * HEADS:(j + 1) * 2 * HEADS], placeT[:, j, :],
                                     vres[:, D:D + 2 * HEADS], start=True, stop=True)
                for j in range(OCT):
                    last = nc.tensor.matmul(pt[:, j // 4, (j % 4) * D:(j % 4 + 1) * D], placeT[:, j, :], vres[:, 0:D],
                                            start=True, stop=True)
                last.then_inc(sent_back, 1)

            def octet(g, last):
                for j in range(OCT):
                    sums(g * OCT + j, j % 2)
                    if j == VAT:
                        overflow_sums(g)
                    if not last or j + 5 < OCT:
                        pack(g * OCT + (j + 5), (j + 1) % 2)
                    if j == 3:
                        overflow_lists(g)
                send_back(g)

            for t in range(len(EARLY), 5):
                pack(t, t % 2)
            pe.nop(nofuse=True).then_inc(summed, FREE)
            with pe.Fori(0, T // OCT - 1) as g:
                octet(g, False)
            octet(T // OCT - 1, True)

            pe.wait_ge(main_done, 1)
            nc.tensor.matmul(po[0:1, 0, 0:T], ones[:, :], rowflag[:, :], start=True, stop=True) \
                .then_inc(flags_counted, 1)
            with pe.If(any_flagged(pe) > 0):
                with pe.Fori(0, T) as t:
                    flag, rank, _ = control(pe, t)
                    with pe.If(flag > 0):
                        pe.wait_ge(degrees_ready, rank + 1)
                        nc.tensor.matmul(po[0:1, 1, 0:P], degree[:, :], ident[:, :], start=True, stop=True) \
                            .then_inc(degrees_turned, 1)

        @block.vector
        def _(dve):
            V = nc.vector
            V.memset(zeros[:, :], 0.0)
            V.memset(neg_tiny[:, :], -1.1754944e-38).then_inc(tiny_set, 1)
            st = Steps(dve, prep_step)
            dve.wait_ge(w_landed, 16 * 5)
            V.tensor_scalar(ablk[:, 0:HEADS], headsel[:, :], acol[:, 0:1], None, ALU.mult)
            V.tensor_scalar(ablk[:, HEADS:2 * HEADS], headsel[:, :], acol[:, 1:2], None, ALU.mult) \
                .then_inc(a_spread, 1)
            dve.wait_ge(w_turned, 2)
            V.tensor_copy(waug[:, 0:D], pt[:, 0, 0:P])
            V.tensor_copy(waug[:, D:RW], pt[:, 1, 0:2 * HEADS]).then_inc(waug_ready, 1)
            dve.wait_ge(cleared, 1)

            def topk(steps, dst, src, spare, imm):
                for r in range(ROUNDS):
                    if r:
                        steps.wait()
                    dve.nop(nofuse=True)
                    steps.done(V.max(dst[:, 8 * r:8 * r + 8], src))
                    if r < ROUNDS - 1:
                        steps.wait()
                        dve.nop(nofuse=True)
                        steps.done(V.match_replace(spare, dst[:, 8 * r:8 * r + 8], src, imm))
                        src = spare

            def extract(t, b):
                ext = Steps(dve, ext_step, t * N_EXT)
                dve.wait_ge(packed, t * NCH + NCH)
                dve.nop(nofuse=True)
                for s in range(NSEG):
                    last = V.max(cand[:, 8 * s:8 * s + 8], keys[:, b, s * SEG:(s + 1) * SEG])
                last.then_inc(keys_read, 1)
                dve.wait_ge(keys_read, t + 1)
                ext.done(V.tensor_reduce(over4[:, b, 0:1], cand[:, 7:CANDS:8], AX, ALU.max))
                topk(ext, words[:, b, :], cand[:, :], cand2[:, :], -1.0)
                assert ext.n == N_EXT
                ext.wait()

            def decode(pair, q, at):
                dec = Steps(dve, dec_step, pair * N_DEC)

                def step(ins):
                    dec.done(ins)
                    dec.wait()

                step(V.tensor_scalar(keyi[:, :, :], words[:, :, :], float(WORDS), None, ALU.mult))
                dec.done(V.tensor_scalar(posi[:, :, :], keyi[:, :, :], WORDS - 1, None, ALU.bitwise_and))
                step(V.tensor_scalar(wi[:, :, :], keyi[:, :, :], WORDS.bit_length() - 1, None,
                                     ALU.logical_shift_right))
                step(V.tensor_copy(wf[:, :, :], wi[:, :, :]))
                for r in range(PEEL):
                    bits = wf[:, :, :].bitcast(I32)
                    dec.done(V.tensor_scalar(topbit[:, :, :], bits, 0x7F800000, None, ALU.bitwise_and))
                    step(V.tensor_scalar(bitno[:, :, :], bits, 23, WORDS.bit_length() - 1,
                                         ALU.logical_shift_right, ALU.logical_shift_left))
                    dec.done(V.tensor_tensor(ents[:, :, r * SLOTS:(r + 1) * SLOTS], bitno[:, :, :], posi[:, :, :],
                                             ALU.add))
                    step(V.tensor_tensor(wf[:, :, :], wf[:, :, :], topbit[:, :, :].bitcast(F32), ALU.subtract))
                own = along(selfid[:, bass.ds(pair * 2, 2)], ENTRIES)
                step(V.tensor_scalar(ents[:, :, :], ents[:, :, :], 1.0 - EXPO, None, ALU.add))
                step(V.tensor_tensor(notself[:, :, :], ents[:, :, :], own, ALU.not_equal))
                step(V.tensor_tensor(ents[:, :, :], ents[:, :, :], notself[:, :, :], ALU.mult))
                for b in range(2):
                    topk(dec, top[:, b, :], ents[:, b, :], ents2[:, b, :], -2.0 * EXPO)
                dec.done(V.tensor_reduce(over4[:, :, 2:3], wf[:, :, :], AX, ALU.max))
                dec.done(V.tensor_copy(over4[:, :, 1:2], words[:, :, SLOTS - 1:SLOTS]))
                dec.wait()
                dec.done(V.tensor_copy(over4[:, :, 3:4], top[:, :, SLOTS - 1:SLOTS]))
                dec.done(V.tensor_scalar(topc[:, :, :], top[:, :, :], 0.0, None, ALU.max))
                dec.done(V.tensor_scalar(inv[:, :, :], top[:, :, :], 0.5, None, ALU.is_lt))
                dec.wait()
                dec.done(V.tensor_reduce(over[:, bass.ds(pair * 2, 2)], over4[:, :, :], AX, ALU.max))
                dec.done(V.tensor_copy(far[:, at:at + 2, 0:OVER], topc[:, :, NEAR:SLOTS]))
                dec.done(V.tensor_copy(far[:, at:at + 2, OVER:OVER + HEADS], H[:, bass.ds(pair * 2, 2), ROW:RW]))
                V.tensor_scalar(moref[:, at:at + 2], top[:, :, NEAR], 0.5, None, ALU.is_gt)
                V.tensor_scalar(more[:, at:at + 2], top[:, :, NEAR], 0.5, None, ALU.is_gt).then_inc(more_made, 1)
                dec.done(V.tensor_scalar(pen[:, q, :, :], inv[:, :, :], NEG, None, ALU.mult))
                step(V.scalar_tensor_tensor(idxf[:, :, :], inv[:, :, :], float(N + 1), topc[:, :, :], ALU.mult,
                                            ALU.add))
                V.tensor_scalar(idx[:, q, :, :], idxf[:, :, :], -1.0, None, ALU.add).then_inc(lists_ready, 1)
                return dec.n

            def stats(i):
                here = slice(i * PIECE, (i + 1) * PIECE)
                dve.wait_ge(x_landed[i], 16)
                st.done(V.tensor_reduce(mean[:, here], X[:, here, :], AX, ALU.add))
                st.wait()
                st.done(V.tensor_scalar(mean[:, here], mean[:, here], 1.0 / D, None, ALU.mult))
                st.wait()
                piece = centred_piece(i % 2)
                if i >= 2:
                    dve.wait_ge(turned, (i - 1) * (PIECE // 4))
                V.tensor_tensor(piece, X[:, here, :], along(mean[:, here], D), ALU.subtract).then_inc(centred, 1)
                dve.wait_ge(squared, 2 * i + 1)
                V.tensor_reduce(stat[:, 0, here], squares, AX, ALU.add).then_inc(sq_read, 1)
                V.tensor_scalar(piece, piece, 0.0, None, ALU.max).then_inc(relu_ready, 1)
                dve.wait_ge(squared, 2 * i + 2)
                V.tensor_reduce(stat[:, 1, here], squares, AX, ALU.add).then_inc(sq_read, 1)

            for i in range(NPIECE):
                stats(i)

            dve.nop(nofuse=True).then_inc(merged, 1)
            dve.wait_ge(const_landed, 16 * 8)
            extract(0, 0)
            extract(1, 1)

            def small(ins):
                st.done(ins)
                st.wait()

            dve.wait_ge(sq_read, 2 * NPIECE)
            V.tensor_scalar(stat[:, 0, :], stat[:, 0, :], 1.0 / D, EPS_LN, ALU.mult, ALU.add).then_inc(stat_ready, 1)
            dve.wait_ge(root_ready, 1)
            rstd, arg, lp, lm, n, a2, poly, tmp = root[:, 0, :], sm[:, 1, :], sm[:, 2, :], sm[:, 3, :], sm[:, 0, :], sm[:, 4, :], sm[:, 5, :], sm[:, 6, :]
            small(V.reciprocal(rstd, rstd))
            small(V.tensor_tensor(n, root[:, 1, :], rstd, ALU.mult))
            small(V.tensor_scalar(n, n, EPS_NORM, None, ALU.max))
            V.tensor_scalar(arg, n, MAX_TANH_ARG, None, ALU.min).then_inc(arg_ready, 1)
            dve.wait_ge(arg_ready, 1)
            small(V.tensor_tensor(a2, arg, arg, ALU.mult))
            small(V.tensor_scalar(poly, a2, 1.0 / 9, 1.0 / 7, ALU.mult, ALU.add))
            for c in (1.0 / 5, 1.0 / 3, 1.0):
                small(V.tensor_tensor(poly, poly, a2, ALU.mult))
                small(V.tensor_scalar(poly, poly, c, None, ALU.add))
            small(V.tensor_tensor(poly, poly, arg, ALU.mult))
            dve.wait_ge(logs_ready, 2)
            small(V.tensor_tensor(lp, lp, lm, ALU.subtract))
            small(V.tensor_scalar(lp, lp, 0.5, None, ALU.mult))
            small(V.tensor_tensor(poly, poly, lp, ALU.subtract))
            small(V.tensor_scalar(tmp, arg, 0.1, None, ALU.is_lt))
            small(V.tensor_tensor(poly, poly, tmp, ALU.mult))
            small(V.tensor_tensor(lp, lp, poly, ALU.add))
            small(V.reciprocal(n, n))
            small(V.tensor_tensor(lp, lp, n, ALU.mult))
            small(V.tensor_tensor(lp, lp, rstd, ALU.mult))
            dve.wait_ge(h_read, QUADS)
            for i in range(NPIECE):
                here = slice(i * PIECE, (i + 1) * PIECE)
                V.tensor_tensor(H[:, here, :], H[:, here, :], along(lp[:, here], RW), ALU.mult).then_inc(scaled, 1)
            dve.wait_ge(scaled, NPIECE)
            decode(0, 0, 0)

            def weigh_logits(g, j, q):
                t, b = g * OCT + j, j % 2
                att = Steps(dve, att_step, t * N_ATT)

                def step(ins):
                    att.done(ins)
                    att.wait()

                own = H[:, bass.ds(t, 1), :]
                e_l = H[:, bass.ds(t, 1), ROW:RW]
                dve.wait_ge(gathered[b], (t - b) * (8 * NEAR) + 16 * NEAR)
                L = lg[:, b, :, :]
                att.done(V.tensor_tensor(L[:, 0:NEAR, :], G[:, b, :, D:ROW],
                                         e_l.broadcast_to([P, NEAR, HEADS]), ALU.add))
                step(V.tensor_tensor(L[:, NEAR:NEAR + 1, :], own[:, :, D:ROW], e_l, ALU.add))
                Lf = L.rearrange("p k h -> p (k h)")
                step(V.scalar_tensor_tensor(Lf, Lf, 0.2, Lf, ALU.mult, ALU.max))
                step(V.tensor_tensor(L[:, 0:NEAR, :], L[:, 0:NEAR, :], along(pen[:, q, b, 0:NEAR], HEADS), ALU.add))
                step(V.tensor_reduce(rowmax[:, j, :], L.rearrange("p k h -> p h k"), AX, ALU.max))
                V.tensor_tensor(L, L, rowmax[:, j:j + 1, :].broadcast_to([P, NEAR + 1, HEADS]),
                                ALU.subtract).then_inc(logits_ready, 1)

            def weigh_rows(g, j):
                t, b = g * OCT + j, j % 2
                dve.wait_ge(probs_ready, t + 1)
                pr = prob[:, b, :, :]
                rows = G[:, b, :, 0:D].rearrange("p k (h d) -> p k h d", h=HEADS)
                V.tensor_tensor(rows, rows, pr[:, 0:NEAR, :].unsqueeze(3)
                                .broadcast_to([P, NEAR, HEADS, HD]), ALU.mult)
                V.tensor_tensor(selfp[:, b, :].rearrange("p (h d) -> p h d", h=HEADS),
                                H[:, bass.ds(t, 1), 0:D].rearrange("p u (h d) -> p (u h) d", h=HEADS),
                                along(pr[:, NEAR, :], HD), ALU.mult).then_inc(weighted, 1)
                V.tensor_reduce(den[:, j, :], pr.rearrange("p k h -> p h k"), AX, ALU.add).then_inc(att_step, 1)

            def overflow_lists(g):
                vl = Steps(dve, vl_step, g * N_VL)

                def step(ins):
                    vl.done(ins)
                    vl.wait()

                vl.done(V.tensor_scalar(nomore[:, :], moref[:, :], -1.0, -NEG, ALU.add, ALU.mult))
                dve.wait_ge(ranked, g + 1)
                step(V.tensor_scalar(dest[:, :], moref[:, :], -4.0 * N, 4.0 * N, ALU.mult, ALU.add))
                step(V.tensor_tensor(dest[:, :], dest[:, :], pt[:, 1, 0:OCT], ALU.add))
                step(V.scalar_tensor_tensor(lost[:, :], dest[:, :], P - 0.5, moref[:, :], ALU.is_gt, ALU.mult))
                flags = over[:, bass.ds(g * OCT, OCT)]
                vl.done(V.tensor_tensor(flags, flags, lost[:, :], ALU.max))
                for j in range(OCT):
                    last = V.tensor_scalar(place[:, j, :], iota_e[:, :], dest[:, j:j + 1], None, ALU.is_equal)
                last.then_inc(placed, 1)
                dve.wait_ge(far_moved, g + 1)
                step(V.tensor_copy(vfar[:, :], pt[:, 1, 16:16 + OVER + HEADS]))
                step(V.tensor_scalar(vinv[:, :], vfar[:, 0:OVER], 0.5, None, ALU.is_lt))
                vl.done(V.tensor_scalar(vpen[:, :], vinv[:, :], NEG, None, ALU.mult))
                step(V.scalar_tensor_tensor(vidxf[:, :], vinv[:, :], float(N + 1), vfar[:, 0:OVER], ALU.mult, ALU.add))
                V.tensor_scalar(vidx[:, :], vidxf[:, :], -1.0, None, ALU.add).then_inc(vlists_ready, 1)
                assert vl.n == N_VL, vl.n

            def overflow_weigh(g):
                va = Steps(dve, vatt_step, g * N_VATT)

                def step(ins):
                    va.done(ins)
                    va.wait()

                dve.wait_ge(vgathered, g * (16 * OVER) + 16 * OVER)
                step(V.tensor_tensor(vlg[:, :, :], GV[:, :, D:ROW],
                                     vfar[:, OVER:OVER + HEADS].unsqueeze(1).broadcast_to([P, OVER, HEADS]),
                                     ALU.add))
                Lf = vlg[:, :, :].rearrange("p k h -> p (k h)")
                step(V.scalar_tensor_tensor(Lf, Lf, 0.2, Lf, ALU.mult, ALU.max))
                step(V.tensor_tensor(vlg[:, :, :], vlg[:, :, :], along(vpen[:, :], HEADS), ALU.add))
                vmax = vres[:, D + HEADS:D + 2 * HEADS]
                step(V.tensor_reduce(vmax, vlg[:, :, :].rearrange("p k h -> p h k"), AX, ALU.max))
                V.tensor_tensor(vlg[:, :, :], vlg[:, :, :], vmax.unsqueeze(1).broadcast_to([P, OVER, HEADS]),
                                ALU.subtract).then_inc(vlogits_ready, 1)
                dve.wait_ge(vprobs_ready, g + 1)
                rows = GV[:, :, 0:D].rearrange("p k (h d) -> p k h d", h=HEADS)
                V.tensor_tensor(rows, rows, vprob[:, :, :].unsqueeze(3).broadcast_to([P, OVER, HEADS, HD]),
                                ALU.mult).then_inc(vweighted, 1)
                va.done(V.tensor_reduce(vres[:, D:D + HEADS], vprob[:, :, :].rearrange("p k h -> p h k"), AX,
                                        ALU.add))
                dve.wait_ge(vsummed, g + 1)
                va.done(V.tensor_copy(vres[:, 0:D], pt[:, 0, 0:D]))
                va.wait()
                dve.nop(nofuse=True).then_inc(vres_ready, 1)
                assert va.n == N_VATT, va.n

            def merge(g):
                me = Steps(dve, merge_step, g * N_MERGE)

                def step(ins):
                    me.done(ins)
                    me.wait()

                def heads(ap):
                    return ap.rearrange("p t (h d) -> p (t h) d", h=HEADS)

                def flat(ap):
                    return ap.rearrange("p t h -> p (t h)")

                dve.wait_ge(sent_back, g + 1)
                back = po[:, 0, 0:OCT * 2 * HEADS].rearrange("p (t c) -> p t c", c=2 * HEADS)
                m1, m2 = m12[:, 0, :, :], m12[:, 1, :, :]
                c1, c2 = c12[:, 0, :, :], c12[:, 1, :, :]
                step(V.tensor_tensor(m2, back[:, :, HEADS:2 * HEADS], along(nomore[:, :], HEADS), ALU.add))
                step(V.tensor_tensor(allmax[:, :, :], rowmax[:, :, :], m2, ALU.max))
                me.done(V.tensor_tensor(m1, rowmax[:, :, :], allmax[:, :, :], ALU.subtract))
                V.tensor_tensor(m2, m2, allmax[:, :, :], ALU.subtract).then_inc(maxima_ready, 1)
                dve.wait_ge(scales_ready, g + 1)
                me.done(V.tensor_tensor(allden[:, :, :], back[:, :, 0:HEADS], c2, ALU.mult))
                step(V.tensor_tensor(den[:, :, :], den[:, :, :], c1, ALU.mult))
                step(V.tensor_tensor(allden[:, :, :], allden[:, :, :], den[:, :, :], ALU.add))
                step(V.reciprocal(allden[:, :, :], allden[:, :, :]))
                me.done(V.tensor_tensor(c1, c1, allden[:, :, :], ALU.mult))
                step(V.tensor_tensor(c2, c2, allden[:, :, :], ALU.mult))
                me.done(V.tensor_tensor(heads(kept[:, :, :]), heads(kept[:, :, :]), along(flat(c1), HD), ALU.mult))
                me.done(V.tensor_tensor(heads(o[:, :, :]), pt[:, :, :].rearrange("p b (c d) -> p (b c) d", d=HD),
                                        along(flat(c2), HD), ALU.mult))
                me.wait()
                V.tensor_tensor(o[:, :, :], o[:, :, :], kept[:, :, :], ALU.add).then_inc(merged, 1)
                assert me.n == N_MERGE, me.n

            def polish(g, part):
                po_ = Steps(dve, pol_step, (g - 1) * N_POL)
                po_.n = (0, 0, 5, 7)[part]

                def step(ins):
                    po_.done(ins)
                    po_.wait()

                if part == 0:
                    dve.wait_ge(merged, g + 1)
                    V.tensor_tensor(o[:, :, :], o[:, :, :], biasb[:, :].unsqueeze(1).broadcast_to([P, OCT, D]),
                                    ALU.add).then_inc(o_ready, 1)
                elif part == 1:
                    dve.wait_ge(expo_ready, g)
                    step(V.tensor_scalar(eo[:, :, :], eo[:, :, :], 1.0, None, ALU.add))
                    step(V.reciprocal(eo[:, :, :], eo[:, :, :]))
                    step(V.tensor_tensor(o[:, :, :], o[:, :, :], eo[:, :, :], ALU.mult))
                    step(V.tensor_tensor(eo[:, :, :], o[:, :, :], o[:, :, :], ALU.mult))
                    step(V.tensor_reduce(nrm[:, :], eo[:, :, :], AX, ALU.add))
                    dve.nop(nofuse=True).then_inc(norms_ready, 1)
                elif part == 2:
                    dve.wait_ge(norms_rooted, g)
                    step(V.tensor_scalar(norm8[:, :], root8[:, :], EPS_NORM, None, ALU.max))
                    dve.nop(nofuse=True).then_inc(norms_kept, 1)
                    po_.done(V.reciprocal(scale8[:, :], norm8[:, :]))
                    po_.wait()
                else:
                    dve.wait_ge(tanh_ready, g)
                    step(V.tensor_tensor(scale8[:, :], scale8[:, :], tanh8[:, :], ALU.mult))
                    step(V.tensor_tensor(o[:, :, :], o[:, :, :], along(scale8[:, :], D), ALU.mult))
                    xs = X[:, bass.ds((g - 1) * OCT, OCT), :]
                    step(V.tensor_tensor(xs, xs, o[:, :, :], ALU.add))
                    dve.nop(nofuse=True).then_inc(out_ready, 1)
                    assert po_.n == N_POL, po_.n

            def octet(g, first, last):
                for j in range(OCT):
                    t = g * OCT + j
                    weigh_logits(g, j, (j // 2) % 2)
                    weigh_rows(g, j)
                    if j == VAT:
                        overflow_weigh(g)
                    if not first and j in POLISH:
                        polish(g, j)
                    if not last or j + 4 < OCT:
                        extract(t + 4, j % 2)
                    if j % 2 and (not last or j + 4 < OCT):
                        decode(g * (OCT // 2) + (j // 2 + 2), (j // 2) % 2, (j + 3) % OCT)
                    if j == 3:
                        overflow_lists(g)
                merge(g)

            for pair in range(1, 2):
                extract(2 * pair, 0)
                extract(2 * pair + 1, 1)
                decode(pair, pair % 2, 2 * pair)
            octet(0, True, False)
            with dve.Fori(1, T // OCT - 1) as g:
                octet(g, False, False)
            octet(T // OCT - 1, False, True)
            for n in range(len(POLISH)):
                polish(T // OCT, n)

            fl = Steps(dve, flags_step)

            def flagstep(ins):
                fl.done(ins)
                fl.wait()

            V.memset(ones[:, :], 1.0)
            V.tensor_scalar(rowflag[:, :], over[:, :], 1.0, None, ALU.is_ge).then_inc(main_done, 1)
            dve.wait_ge(flags_counted, 1)
            flagstep(V.tensor_scalar(flagrow[:, :], po[0:1, 0, 0:T], 0.5, None, ALU.is_gt))
            flagstep(V.tensor_reduce(anyflag[:, :], flagrow[:, :], AX, ALU.add))
            V.tensor_copy(anyi[:, :], anyflag[:, :]).then_inc(any_ready, 1)

            def slow_tile(t, rank, base):
                SLOW, ROUND = 12, 19
                sl = Steps(dve, slow_step, rank * SLOW, apart=True)

                def step(ins):
                    sl.done(ins)
                    sl.wait()

                heads = "p (h d) -> p h d"
                e_l = H[:, bass.ds(t, 1), ROW:RW]
                dve.wait_ge(slow_adj, rank * 48 + 48)
                step(V.scalar_tensor_tensor(slow_keys, slow_keys, 0.0, colid, ALU.is_gt, ALU.mult))
                step(V.scalar_tensor_tensor(slow_keys, colid, selfid[:, bass.ds(t, 1)], slow_keys, ALU.not_equal,
                                            ALU.mult))
                V.tensor_scalar(signs[:, :, :].rearrange("p c n -> p (c n)"), slow_keys, 0.5, None, ALU.is_gt,
                                ALU.add, accum_out=degree[:, :]).then_inc(degrees_ready, 1)
                dve.wait_ge(degrees_turned, rank + 1)
                step(V.tensor_reduce(maxdeg[:, :], po[0:1, 1, 0:P], AX, ALU.max))
                step(V.tensor_scalar(degi[:, :], maxdeg[:, :], 7.0, None, ALU.add))
                step(V.tensor_scalar(rounds[0:1, bass.ds(t, 1)], degi[:, :], 3, None, ALU.logical_shift_right))
                step(V.tensor_copy(maxdeg[:, :], rounds[0:1, bass.ds(t, 1)]))
                step(V.tensor_tensor(tally[0:1, bass.ds(t + 1, 1), 1], tally[0:1, bass.ds(t + 1, 1), 1], maxdeg[:, :],
                                     ALU.add))
                step(V.tensor_tensor(oldmax[:, :], slow_own[:, D:ROW], e_l[:, 0, :], ALU.add))
                step(V.scalar_tensor_tensor(oldmax[:, :], oldmax[:, :], 0.2, oldmax[:, :], ALU.mult, ALU.max))
                sl.done(V.memset(den8[:, :], 1.0))
                V.tensor_copy(acc[:, :], slow_own[:, 0:D]).then_inc(rounds_ready, 1)
                count = round_count(dve, t, rank)
                for r in round_loop(dve, count):
                    with dve.If(r < count):
                        n = base + r
                        rs = Steps(dve, round_step, n * ROUND, apart=True)

                        def rstep(ins):
                            rs.done(ins)
                            rs.wait()

                        rstep(V.max(top8[:, :], slow_keys))
                        dve.nop(nofuse=True)
                        rs.done(V.match_replace(slow_keys, top8[:, :], slow_keys, 0.0))
                        rstep(V.tensor_scalar(inv8[:, :], top8[:, :], 0.5, None, ALU.is_lt))
                        rs.done(V.tensor_scalar(pen8[:, :], inv8[:, :], NEG, None, ALU.mult))
                        rstep(V.scalar_tensor_tensor(idxf8[:, :], inv8[:, :], float(N + 1), top8[:, :], ALU.mult,
                                                     ALU.add))
                        V.tensor_scalar(idx8[:, :], idxf8[:, :], -1.0, None, ALU.add).then_inc(round_lists, 1)
                        dve.wait_ge(round_gathered, n * 128 + 128)
                        L = lg8[:, 0:8, :]
                        rstep(V.tensor_tensor(L, G[:, 0, 0:8, D:ROW], e_l.broadcast_to([P, 8, HEADS]), ALU.add))
                        rstep(V.scalar_tensor_tensor(L, L, 0.2, L, ALU.mult, ALU.max))
                        rstep(V.tensor_tensor(L, L, along(pen8[:, :], HEADS), ALU.add))
                        rstep(V.tensor_reduce(rmax8[:, :], L.rearrange("p k h -> p h k"), AX, ALU.max))
                        rs.done(V.tensor_tensor(newmax[:, :], oldmax[:, :], rmax8[:, :], ALU.max))
                        rstep(V.tensor_copy(lg8[:, 8, :], oldmax[:, :]))
                        V.tensor_tensor(lg8[:, :, :], lg8[:, :, :],
                                        newmax[:, :].unsqueeze(1).broadcast_to([P, 9, HEADS]),
                                        ALU.subtract).then_inc(round_logits, 1)
                        rs.done(V.tensor_copy(oldmax[:, :], newmax[:, :]))
                        dve.wait_ge(round_probs, n + 1)
                        rs.done(V.tensor_reduce(sum8[:, :], prob8[:, 0:8, :].rearrange("p k h -> p h k"), AX,
                                                ALU.add))
                        rstep(V.tensor_tensor(den8[:, :], den8[:, :], prob8[:, 8, :], ALU.mult))
                        rs.done(V.tensor_tensor(den8[:, :], den8[:, :], sum8[:, :], ALU.add))
                        rows = G[:, 0, 0:8, 0:D].rearrange("p k (h d) -> p k h d", h=HEADS)
                        rstep(V.tensor_tensor(rows, rows, prob8[:, 0:8, :].unsqueeze(3)
                                              .broadcast_to([P, 8, HEADS, HD]), ALU.mult))
                        rs.done(V.tensor_reduce(part[:, :], G[:, 0, 0:8, 0:D].rearrange("p k d -> p d k"), AX,
                                                ALU.add))
                        av = acc[:, :].rearrange(heads, h=HEADS)
                        rstep(V.tensor_tensor(av, av, along(prob8[:, 8, :], HD), ALU.mult))
                        rstep(V.tensor_tensor(acc[:, :], acc[:, :], part[:, :], ALU.add))
                        assert rs.n == ROUND, rs.n
                step(V.reciprocal(den8[:, :], den8[:, :]))
                step(V.tensor_tensor(o[:, 0, :].rearrange(heads, h=HEADS), acc[:, :].rearrange(heads, h=HEADS),
                                     along(den8[:, :], HD), ALU.mult))
                V.tensor_tensor(o[:, 0, :], o[:, 0, :], biasb[:, :], ALU.add).then_inc(slow_o, 1)
                assert sl.n == SLOW, sl.n
                dve.wait_ge(slow_expo, rank + 1)
                tail = Steps(dve, tail_step, rank * 8, apart=True)

                def tstep(ins):
                    tail.done(ins)
                    tail.wait()

                z = o[:, 0, :]
                tstep(V.tensor_scalar(eo[:, 0, :], eo[:, 0, :], 1.0, None, ALU.add))
                tstep(V.reciprocal(eo[:, 0, :], eo[:, 0, :]))
                tstep(V.tensor_tensor(z, z, eo[:, 0, :], ALU.mult))
                tstep(V.tensor_tensor(eo[:, 1, :], z, z, ALU.mult))
                V.tensor_reduce(nrm[:, 0:1], eo[:, 1, :], AX, ALU.add).then_inc(slow_nrm, 1)
                dve.wait_ge(slow_root, rank + 1)
                V.tensor_scalar(norm8[:, 0:1], root8[:, 0:1], EPS_NORM, None, ALU.max).then_inc(slow_norm, 1)
                dve.wait_ge(slow_norm, rank + 1)
                tstep(V.reciprocal(scale8[:, 0:1], norm8[:, 0:1]))
                dve.wait_ge(slow_tanh, rank + 1)
                tstep(V.tensor_tensor(scale8[:, 0:1], scale8[:, 0:1], tanh8[:, 0:1], ALU.mult))
                tstep(V.tensor_scalar(z, z, scale8[:, 0:1], None, ALU.mult))
                tstep(V.tensor_tensor(slow_out, slow_x, z, ALU.add))
                assert tail.n == 8
                dve.nop(nofuse=True).then_inc(slow_out_ready, 1)
                dve.wait_ge(slow_stored, rank * 16 + 16)
                dve.nop(nofuse=True).then_inc(slow_free, 1)

            with dve.If(any_flagged(dve) > 0):
                fl.done(V.memset(tally[:, :, :], 0.0))
                fl.wait()
                V.drain().then_inc(slow_free, 1)
                dve.wait_ge(colid_landed, 16)
                with dve.Fori(0, T) as t:
                    tl = Steps(dve, tally_step, t * 3, apart=True)
                    tl.done(V.tensor_tensor(tally[0:1, bass.ds(t + 1, 1), 0], tally[0:1, bass.ds(t, 1), 0],
                                            flagrow[0:1, bass.ds(t, 1)], ALU.add))
                    tl.done(V.tensor_copy(tally[0:1, bass.ds(t + 1, 1), 1], tally[0:1, bass.ds(t, 1), 1]))
                    tl.done(V.tensor_copy(ctl[0:1, bass.ds(t, 1), 0], flagrow[0:1, bass.ds(t, 1)]))
                    tl.wait()
                    V.tensor_copy(ctl[0:1, bass.ds(t, 1), 1:3], tally[0:1, bass.ds(t, 1), :]).then_inc(ctl_ready, 1)
                    flag, rank, base = control(dve, t)
                    with dve.If(flag > 0):
                        slow_tile(t, rank, base)


def kernel(x, adj, L0_gnn_W, L0_gnn_a_l, L0_gnn_a_r, L0_gnn_bias):
    import numpy as np
    import ml_dtypes
    import concourse.bacc as bacc
    from concourse.bass_utils import run_bass_kernel_spmd

    N = 8192
    W = N // BITS
    pos = np.arange(W)
    packw = np.zeros((P, BITS, P), np.float32)
    packw[np.arange(P), :, np.arange(P)] = 2.0 ** (np.arange(BITS) - 1)
    consts = {
        "ident": np.eye(P, dtype=np.float32),
        "packw": packw.astype(ml_dtypes.bfloat16),
        "posrow": np.stack([np.full(W, (2 ** BITS - 1) / 2), (pos // 32 * 32) / W, (pos % 32) / W]).astype(ml_dtypes.bfloat16),
        "onesrow": np.ones((3, P), ml_dtypes.bfloat16),
        "selfid": (np.arange(P)[:, None] + P * np.arange(N // P)[None, :] + 1).astype(np.float32),
        "headsel": (np.arange(P)[:, None] // (P // HEADS) == np.arange(HEADS)[None, :]).astype(np.float32),
        "colid": np.arange(1, N + 1, dtype=np.float32)[None, :],
        "ltri": np.triu(np.ones((P, P)), 1).astype(ml_dtypes.bfloat16),
        "allones": np.ones((P, P), ml_dtypes.bfloat16),
        "iota_e": np.broadcast_to(np.arange(P, dtype=np.float32), (P, P)),
    }
    nc = bacc.Bacc("TRN2", target_bir_lowering=False, num_devices=1)
    arrays = {"x": x, "adj": adj, "W": L0_gnn_W, "a_l": L0_gnn_a_l, "a_r": L0_gnn_a_r, "bias": L0_gnn_bias, **consts}
    args, feed = [], {}
    for name, a in arrays.items():
        a = np.ascontiguousarray(a)
        feed[f"in_{name}"] = a
        args.append(nc.dram_tensor(f"in_{name}", a.shape, mybir.dt.from_np(a.dtype), kind="ExternalInput").ap())
    args.append(nc.dram_tensor("out", (N, P), F32, kind="ExternalOutput").ap())
    build(nc, *args)
    r = run_bass_kernel_spmd(nc, [feed], core_ids=[0])
    return r.results[0]["out"]
```

```python
from contextlib import ExitStack

import concourse.bass as bass
from concourse import mybir

P = 128
ALU = mybir.AluOpType
ACT = mybir.ActivationFunctionType
AX = mybir.AxisListType.X
F32 = mybir.dt.float32
BF16 = mybir.dt.bfloat16
I32 = mybir.dt.int32
U32 = mybir.dt.uint32

HEADS = 4
BITS = 8
SEG = 64
SLOTS = 24
NEAR = 12
OCT = 8
ROUNDS = SLOTS // 8
PEEL = 3
CHUNK = 2048
MAX_TANH_ARG = 1.0 - 1e-05
EPS_LN = 1e-05
EPS_NORM = 1e-15
NEG = -1e30


class Steps:

    def __init__(self, eng, sem, base=0, apart=False):
        self.eng, self.sem, self.base, self.n, self.apart = eng, sem, base, 0, apart

    def done(self, ins):
        self.n += 1
        ins.then_inc(self.sem, 1)

    def wait(self):
        self.eng.wait_ge(self.sem, self.base + self.n)
        if self.apart:
            self.eng.nop(nofuse=True)


def build(nc, x, adj, W, a_l, a_r, bias, ident_d, packw_d, posrow_d, onesrow_d, selfid_d, headsel_d, colid_d, ltri_d,
          allones_d, iota_e_d, out):
    N, D = x.shape
    T = N // P
    PAIRS = T // 2
    WORDS = N // BITS
    NCH = N // CHUNK
    BPC = CHUNK // WORDS
    NSEG = WORDS // SEG
    CANDS = NSEG * 8
    HD = D // HEADS
    ROW = D + HEADS
    RW = ROW + HEADS
    PIECE = 16
    NPIECE = T // PIECE
    QUADS = T // 4
    EXPO = 127 * WORDS
    ENTRIES = PEEL * SLOTS
    N_WORDS, N_DEC, N_ATT, N_VL, N_VATT, N_MERGE = 21, 74, 4, 10, 4, 10
    N_POL = 6
    POLISH = (1, 2, 3, 4, 5)
    POLISH_ACT = (1, 2, 3, 4, 6)
    HELD_PAIR = 4
    V_PIECES = 2
    OVER = SLOTS - NEAR
    AHEAD = 8
    RING = 3
    FREE = 2

    table = nc.dram_tensor("table", (N, ROW), F32, kind="Internal").ap()

    with ExitStack() as ctx:
        def sb(name, shape, dt=F32):
            return ctx.enter_context(nc.sbuf_tensor(name, shape, dt))

        def ps(name, shape, dt=F32):
            return ctx.enter_context(nc.psum_tensor(name, shape, dt))

        def sem(name):
            return ctx.enter_context(nc.semaphore(name))

        ident = sb("ident", [P, P])
        packw = sb("packw", [P, BITS, P], BF16)
        posrow = sb("posrow", [3, WORDS], BF16)
        onesrow = sb("onesrow", [3, P], BF16)
        selfid = sb("selfid", [P, T])
        headsel = sb("headsel", [P, HEADS])
        biasb = sb("biasb", [P, D])
        neg_tiny = sb("neg_tiny", [P, 1])
        acol = sb("acol", [P, 2])
        ablk = sb("ablk", [P, 2 * HEADS])
        waug = sb("waug", [P, RW])
        X = sb("X", [P, T, D])
        H = sb("H", [P, T, RW])
        adjbuf = sb("adjbuf", [P, 2, NCH, CHUNK])
        signs = sb("signs", [P, NCH, CHUNK], BF16)
        GG = sb("GG", [P, RING * NEAR, ROW])
        G = GG[:, :, :].rearrange("p (b k) r -> p b k r", b=RING)
        GV = G[:, OCT % RING, :, :]
        mean = sb("mean", [P, T])
        factor = mean
        stat = sb("stat", [P, 2, T])
        root = sb("root", [P, 2, T])
        sm = sb("sm", [P, 8, T])
        rT = sb("rT", [P, 2, 512])
        cand = sb("cand", [P, 4, CANDS])
        wraw = cand[:, 0, :]
        cand2 = sm[:, :, :].rearrange("p (t a) n -> p t (a n)", t=4)
        words = sb("words", [P, 4, SLOTS])
        keyi = sb("keyi", [P, 4, SLOTS], I32)
        posi = sb("posi", [P, 4, SLOTS], I32)
        wi = sb("wi", [P, 4, SLOTS], I32)
        wf = sb("wf", [P, 4, SLOTS])
        topbit = sb("topbit", [P, 4, SLOTS], I32)
        bitno = sb("bitno", [P, 4, SLOTS], I32)
        ents = sb("ents", [P, 4, ENTRIES])
        ents2 = cand2[:, :, 0:ENTRIES]
        top = sb("top", [P, 4, SLOTS])
        topc = sb("topc", [P, 4, SLOTS])
        inv = sb("inv", [P, 4, SLOTS])
        pen = sb("pen", [P, 4, NEAR])
        idxf = sb("idxf", [P, 4, NEAR])
        idx = sb("idx", [P, 2, 4, NEAR], U32)
        maskel = sb("maskel", [P, 2, 4, NEAR, HEADS])
        over4 = sb("over4", [P, 4, 4])
        selfl = sb("selfl", [P, T, HEADS])
        over = sb("over", [P, T])
        lg = sb("lg", [P, 2, NEAR + 1, HEADS])
        prob = sb("prob", [P, 2, NEAR + 1, HEADS])
        rowmax = sb("rowmax", [P, OCT + 1, HEADS])
        den = sb("den", [P, OCT + 2, HEADS])
        kept_o = sb("kept_o", [P, 2, OCT, D])
        kept = kept_o[:, 0, :, :]
        o = kept_o[:, 1, :, :]
        ltri = sb("ltri", [P, P], BF16)
        allones = sb("allones", [P, P], BF16)
        iota_e = sb("iota_e", [P, P])
        zeros = sb("zeros", [P, OCT], BF16)
        more = sb("more", [P, OCT], BF16)
        moref = sb("moref", [P, OCT])
        nomore = sb("nomore", [P, OCT])
        dest = sb("dest", [P, OCT])
        lost = sb("lost", [P, OCT])
        far = sb("far", [P, OCT, OVER + HEADS])
        place = sb("place", [P, OCT, P])
        placeT = rT[:, :, :].rearrange("p b n -> p (b n)").rearrange("p (t e) -> p t e", e=P)
        vfar = sb("vfar", [P, OVER + HEADS])
        vinv = sb("vinv", [P, OVER])
        vidxf = sb("vidxf", [P, OVER])
        vidx = sb("vidx", [P, OVER], U32)
        vpen = sb("vpen", [P, OVER])
        vmaskel = sb("vmaskel", [P, OVER, HEADS])
        vlg = sb("vlg", [P, OVER, HEADS])
        vprob = sb("vprob", [P, OVER, HEADS])
        vres = sb("vres", [P, D + 2 * HEADS])
        back = sb("back", [P, OCT, 2 * HEADS])
        m12 = sb("m12", [P, 2, OCT, HEADS])
        c12 = sb("c12", [P, 2, OCT, HEADS])
        allmax = sb("allmax", [P, OCT, HEADS])
        allden = sb("allden", [P, OCT, HEADS])
        selfp = sb("selfp", [P, 2, D])
        eo = place
        nrm = sb("nrm", [P, OCT])
        root8 = sb("root8", [P, OCT])
        norm8 = sb("norm8", [P, OCT])
        tanh8 = sb("tanh8", [P, OCT])
        scale8 = sb("scale8", [P, OCT])

        ones = sb("ones", [P, 1])
        rowflag = sb("rowflag", [P, T])
        spare = cand[0:1, :, :].rearrange("p t n -> p (t n)")
        flagrow = spare[:, 0:T]
        anyflag = sb("anyflag", [1, 1])
        anyi = sb("anyi", [1, 1], I32)
        tally = spare[:, T:3 * T + 2].rearrange("p (t c) -> p t c", c=2)
        ctl = spare[:, 4 * T:7 * T].bitcast(I32).rearrange("p (t c) -> p t c", c=3)
        degree = sb("degree", [P, 1])
        maxdeg = sb("maxdeg", [1, 1])
        degi = sb("degi", [1, 1], I32)
        rounds = spare[:, 7 * T:8 * T].bitcast(I32)
        top8 = sb("top8", [P, 8])
        inv8 = sb("inv8", [P, 8])
        idxf8 = sb("idxf8", [P, 8])
        idx8 = sb("idx8", [P, 8], U32)
        pen8 = sb("pen8", [P, 8])
        lg8 = sb("lg8", [P, 9, HEADS])
        prob8 = sb("prob8", [P, 9, HEADS])
        newmax = sb("newmax", [P, HEADS])
        oldmax = sb("oldmax", [P, HEADS])
        rmax8 = sb("rmax8", [P, HEADS])
        den8 = sb("den8", [P, HEADS])
        sum8 = sb("sum8", [P, HEADS])
        acc, part = kept[:, 2, :], kept[:, 3, :]

        keys = ps("keys", [P, 2, WORDS])
        po = ps("po", [P, 2, 512])
        pt = ps("pt", [P, 2, 512])

        x_landed = [sem(f"x_landed{i}") for i in range(NPIECE)]
        w_landed = sem("w_landed")
        const_landed = sem("const_landed")
        adj_landed = [sem(f"adj_landed{i}") for i in range(2 * NCH)]
        cleared = sem("cleared")
        tiny_set = sem("tiny_set")
        w_turned = sem("w_turned")
        a_spread = sem("a_spread")
        waug_ready = sem("waug_ready")
        means_ready = sem("means_ready")
        centred = sem("centred")
        centred_squared = sem("centred_squared")
        relu_squared = sem("relu_squared")
        relu_ready = sem("relu_ready")
        centred_summed = sem("centred_summed")
        relu_summed = sem("relu_summed")
        turned = sem("turned")
        rT_ready = sem("rT_ready")
        h_done = sem("h_done")
        h_read = sem("h_read")
        prep_step = sem("prep_step")
        stat_ready = sem("stat_ready")
        root_ready = sem("root_ready")
        arg_ready = sem("arg_ready")
        logs_ready = sem("logs_ready")
        scaled = sem("scaled")
        scaled_pool = sem("scaled_pool")
        factors_ready = sem("factors_ready")
        table_stored = sem("table_stored")
        signed = sem("signed")
        packed = sem("packed")
        keys_read = sem("keys_read")
        dec_step = sem("dec_step")
        lists_ready = sem("lists_ready")
        gathered = [sem(f"gathered{b}") for b in range(RING)]
        att_step = sem("att_step")
        dens_made = sem("dens_made")
        logits_ready = sem("logits_ready")
        probs_ready = sem("probs_ready")
        weighted = sem("weighted")
        summed = sem("summed")
        sums_kept = sem("sums_kept")
        more_made = sem("more_made")
        ranked = sem("ranked")
        vl_step = sem("vl_step")
        placed = sem("placed")
        far_moved = sem("far_moved")
        place_turned = sem("place_turned")
        placeT_ready = sem("placeT_ready")
        vlists_ready = sem("vlists_ready")
        vatt_step = sem("vatt_step")
        vlogits_ready = sem("vlogits_ready")
        vprobs_ready = sem("vprobs_ready")
        vweighted = sem("vweighted")
        vsummed = sem("vsummed")
        vres_ready = sem("vres_ready")
        sent_back = sem("sent_back")
        merge_step = sem("merge_step")
        pol_step = sem("pol_step")
        maxima_ready = sem("maxima_ready")
        scales_ready = sem("scales_ready")
        merged = sem("merged")
        back_kept = sem("back_kept")
        o_ready = sem("o_ready")
        sigmoid_ready = sem("sigmoid_ready")
        silu_ready = sem("silu_ready")
        o_squared = sem("o_squared")
        norms_ready = sem("norms_ready")
        norms_rooted = sem("norms_rooted")
        norms_kept = sem("norms_kept")
        tanh_ready = sem("tanh_ready")
        flags_step = sem("flags_step")
        flags_counted = sem("flags_counted")
        any_ready = sem("any_ready")
        ctl_ready = sem("ctl_ready")
        colid_landed = sem("colid_landed")
        slow_free = sem("slow_free")
        slow_adj = sem("slow_adj")
        slow_step = sem("slow_step")
        degrees_ready = sem("degrees_ready")
        degrees_turned = sem("degrees_turned")
        rounds_ready = sem("rounds_ready")
        round_step = sem("round_step")
        round_lists = sem("round_lists")
        round_gathered = sem("round_gathered")
        round_logits = sem("round_logits")
        round_probs = sem("round_probs")
        slow_o = sem("slow_o")
        slow_sigmoid = sem("slow_sigmoid")
        main_done = sem("main_done")
        tally_step = sem("tally_step")
        tail_step = sem("tail_step")
        slow_nrm = sem("slow_nrm")
        slow_root = sem("slow_root")
        slow_norm = sem("slow_norm")
        slow_tanh = sem("slow_tanh")
        slow_out_ready = sem("slow_out_ready")
        slow_stored = sem("slow_stored")
        out_ready = sem("out_ready")
        out_stored = sem("out_stored")

        SPAN = PIECE * D
        GGflat = GG[:, :, :].rearrange("p k r -> p (k r)")
        halves = (kept_o[:, :, :, :].rearrange("p a t c -> p (a t c)"), GGflat)

        def centred_piece(b):
            return halves[b][:, 0:SPAN].rearrange("p (t c) -> p t c", c=D)

        squares = GGflat[:, SPAN:2 * SPAN].rearrange("p (t c) -> p t c", c=D)

        def relu_squares(i):
            if i == NPIECE - 1:
                return squares
            return H[:, (NPIECE - 1) * PIECE:T, :].rearrange("p t c -> p (t c)")[:, 0:SPAN] \
                .rearrange("p (t c) -> p t c", c=D)

        x_t = x.rearrange("(t p) c -> p t c", p=P)
        out_t = out.rearrange("(t p) c -> p t c", p=P)
        table_t = table.rearrange("(t p) c -> p t c", p=P)

        def along(ap, n):
            return ap.unsqueeze(2).broadcast_to([ap.shape[0], ap.shape[1], n])

        colid = adjbuf[:, 1, :, :].rearrange("p c n -> p (c n)")
        slow_keys = adjbuf[:, 0, :, :].rearrange("p c n -> p (c n)")
        slow_own = G[:, 1, 0, :]
        slow_x, slow_out = kept[:, 0, :], kept[:, 1, :]
        MAXROUNDS = N // 8

        def any_flagged(eng):
            eng.wait_ge(any_ready, 1)
            eng.nop(nofuse=True)
            return eng.value_load(anyi[0:1, 0:1], min_val=0, max_val=T)

        def control(eng, t):
            eng.wait_ge(ctl_ready, t + 1)
            eng.nop(nofuse=True)
            flag = eng.value_load(ctl[0:1, bass.ds(t, 1), 0], min_val=0, max_val=1)
            rank = eng.value_load(ctl[0:1, bass.ds(t, 1), 1], min_val=0, max_val=T)
            base = eng.value_load(ctl[0:1, bass.ds(t, 1), 2], min_val=0, max_val=T * MAXROUNDS)
            return flag, rank, base

        def round_count(eng, t, rank):
            eng.wait_ge(rounds_ready, rank + 1)
            eng.nop(nofuse=True)
            return eng.value_load(rounds[0:1, bass.ds(t, 1)], min_val=0, max_val=MAXROUNDS)

        def round_loop(eng, count):
            with eng.Fori(0, MAXROUNDS, 32) as r0:
                with eng.If(r0 < count):
                    with eng.Fori(0, 32) as r1:
                        yield r0 + r1

        def exists(t):
            return not isinstance(t, int) or t < T

        block = ctx.enter_context(nc.Block())

        @block.sync
        def _(sp):
            def load_adj(t, b, c):
                sp.dma_start(adjbuf[:, b, c, :], adj[bass.ds(t * P, P), c * CHUNK:(c + 1) * CHUNK]) \
                    .then_inc(adj_landed[b * NCH + c], 16)

            for i in range(NPIECE):
                sp.dma_start(X[:, i * PIECE:(i + 1) * PIECE, :], x_t[:, i * PIECE:(i + 1) * PIECE, :]) \
                    .then_inc(x_landed[i], 16)
                if i == 0:
                    for dst, src in ((wraw[:, :], W), (acol[:, 0:1], a_r.rearrange("h (d u) -> (h d) u", u=1)),
                                     (acol[:, 1:2], a_l.rearrange("h (d u) -> (h d) u", u=1)),
                                     (ident[:, :], ident_d), (headsel[:, :], headsel_d)):
                        sp.dma_start(dst, src).then_inc(w_landed, 16)
            for dst, src in ((packw[:, :, :], packw_d), (posrow[:, :], posrow_d), (onesrow[:, :], onesrow_d),
                             (selfid[:, :], selfid_d), (ltri[:, :], ltri_d), (allones[:, :], allones_d),
                             (iota_e[:, :], iota_e_d),
                             (biasb[:, :], bias.unsqueeze(0).broadcast_to([P, D]))):
                sp.dma_start(dst, src).then_inc(const_landed, 16)
            for t in range(2):
                for c in range(NCH):
                    load_adj(t, t, c)
            def load_pair(pair):
                for b in range(2):
                    for c in range(NCH):
                        sp.wait_ge(signed, pair * (2 * NCH) + (b * NCH + c + 1 - 2 * NCH))
                        load_adj(pair * 2 + b, b, c)

            for pair in range(1, HELD_PAIR):
                load_pair(pair)
            sp.wait_ge(table_stored, 16 * NPIECE)
            with sp.Fori(HELD_PAIR, PAIRS) as pair:
                load_pair(pair)
            with sp.If(any_flagged(sp) > 0):
                sp.dma_start(colid, colid_d.broadcast_to([P, N])).then_inc(colid_landed, 16)
                with sp.Fori(0, T) as t:
                    flag, rank, _ = control(sp, t)
                    with sp.If(flag > 0):
                        sp.wait_ge(slow_free, rank + 1)
                        sp.dma_start(slow_keys, adj[bass.ds(t * P, P), :]).then_inc(slow_adj, 16)
                        sp.dma_start(slow_own, table[bass.ds(t * P, P), :]).then_inc(slow_adj, 16)
                        sp.dma_start(slow_x, x[bass.ds(t * P, P), :]).then_inc(slow_adj, 16)
                        sp.wait_ge(out_stored, 16 * (T // OCT))
                        sp.wait_ge(slow_out_ready, rank + 1)
                        sp.dma_start(out[bass.ds(t * P, P), :], slow_out).then_inc(slow_stored, 16)
                        sp.wait_ge(slow_stored, rank * 16 + 16)
                        sp.nop(nofuse=True)
            sp.wait_ge(out_stored, 16 * (T // OCT))

        @block.gpsimd
        def _(pool):
            nc.gpsimd.memset(GGflat[:, :], 0.0).then_inc(cleared, 1)
            pool.wait_ge(cleared, 1)

            def centre(i):
                here = slice(i * PIECE, (i + 1) * PIECE)
                pool.wait_ge(means_ready, i + 1)
                if i >= 2:
                    pool.wait_ge(turned, (i - 1) * (PIECE // 4))
                    pool.wait_ge(relu_squared, i - 1)
                nc.gpsimd.tensor_tensor(centred_piece(i % 2), X[:, here, :], along(mean[:, here], D), ALU.subtract) \
                    .then_inc(centred, 1)

            def square_centred(i):
                pool.wait_ge(centred, i + 1)
                if i:
                    pool.wait_ge(centred_summed, i)
                piece = centred_piece(i % 2)
                nc.gpsimd.tensor_tensor(squares, piece, piece, ALU.mult).then_inc(centred_squared, 1)

            def square_clipped(i):
                pool.wait_ge(relu_ready, i + 1)
                if i:
                    pool.wait_ge(relu_summed, i)
                piece = centred_piece(i % 2)
                nc.gpsimd.tensor_tensor(relu_squares(i), piece, piece, ALU.mult).then_inc(relu_squared, 1)

            centre(0)
            square_centred(0)
            centre(1)
            for i in range(NPIECE):
                if i % 2 == 0:
                    square_clipped(i)
                if i + 1 < NPIECE:
                    square_centred(i + 1)
                if i + 2 < NPIECE:
                    centre(i + 2)

            def store(i):
                pool.dma_start(table_t[:, i * PIECE:(i + 1) * PIECE, :], H[:, i * PIECE:(i + 1) * PIECE, 0:ROW]) \
                    .then_inc(table_stored, 16)

            pool.wait_ge(factors_ready, 1)
            pool.wait_ge(h_read, QUADS)
            for n, i in enumerate(range(V_PIECES, NPIECE)):
                here = slice(i * PIECE, (i + 1) * PIECE)
                nc.gpsimd.tensor_tensor(H[:, here, :], H[:, here, :], along(factor[:, here], RW), ALU.mult) \
                    .then_inc(scaled_pool, 1)
                pool.wait_ge(scaled_pool, n + 1)
                store(i)
            for i in range(V_PIECES):
                pool.wait_ge(scaled, i + 1)
                store(i)
            pool.wait_ge(table_stored, 16 * NPIECE)

            def fetch(buf, index, done):
                for k in range(NEAR):
                    nc.gpsimd.indirect_dma_start(
                        buf[:, k, :], None, table, bass.IndirectOffsetOnAxis(ap=index[:, k:k + 1], axis=0),
                        bounds_check=N - 1, oob_is_err=False).then_inc(done, 16)

            with pool.Fori(0, T // OCT) as g:
                for i in range(OCT):
                    if i % 4 == 0:
                        pool.wait_ge(lists_ready, g * 2 + (i // 4 + 1))
                    if i == RING - 1:
                        pool.wait_ge(vsummed, g + 1)
                    else:
                        pool.wait_ge(summed, g * OCT + (i - RING + (1 if i >= RING else 2) + FREE))
                    pool.nop(nofuse=True)
                    fetch(G[:, i % RING, :, :], idx[:, i // 4, i % 4, :], gathered[i % RING])
                pool.wait_ge(vlists_ready, g + 1)
                pool.wait_ge(summed, g * OCT + (OCT - RING + 1 + FREE))
                pool.nop(nofuse=True)
                fetch(GV, vidx[:, :], gathered[OCT % RING])

            with pool.If(any_flagged(pool) > 0):
                with pool.Fori(0, T) as t:
                    flag, rank, base = control(pool, t)
                    with pool.If(flag > 0):
                        count = round_count(pool, t, rank)
                        for r in round_loop(pool, count):
                            with pool.If(r < count):
                                pool.wait_ge(round_lists, base + r + 1)
                                pool.nop(nofuse=True)
                                for k in range(8):
                                    nc.gpsimd.indirect_dma_start(
                                        G[:, 0, k, :], None, table,
                                        bass.IndirectOffsetOnAxis(ap=idx8[:, k:k + 1], axis=0),
                                        bounds_check=N - 1, oob_is_err=False).then_inc(round_gathered, 16)

        @block.scalar
        def _(act):
            def sign(t, b, first=False, chunks=range(NCH)):
                for c in chunks:
                    act.wait_ge(adj_landed[b * NCH + c], (t - b) * 8 + 16)
                    if not first:
                        act.wait_ge(packed, t * NCH + (c + 1 - NCH))
                    nc.scalar.activation(signs[:, c, :], adjbuf[:, b, c, :], ACT.Sign, bias=neg_tiny[:, :]) \
                        .then_inc(signed, 1)

            def keep(quad):
                act.wait_ge(h_done, quad + 1)
                for j in range(2):
                    last = nc.scalar.copy(H[:, 4 * quad + 2 * j:4 * quad + 2 * j + 2, :],
                                          po[:, j, 0:2 * RW].rearrange("p (t c) -> p t c", c=RW))
                last.then_inc(h_read, 1)

            act.wait_ge(tiny_set, 1)
            for quad in range(QUADS):
                act.wait_ge(turned, quad + 1)
                if quad >= 2:
                    act.wait_ge(h_done, quad - 1)
                nc.scalar.copy(rT[:, quad % 2, :], pt[:, quad % 2, :]).then_inc(rT_ready, 1)
                if quad:
                    keep(quad - 1)
                t = quad // NCH
                sign(t, t % 2, t == 0, (quad % NCH,))
                if quad == QUADS - 3:
                    act.wait_ge(stat_ready, 1)
                    nc.scalar.activation(root[:, :, :], stat[:, :, :], ACT.Sqrt).then_inc(root_ready, 1)
                if quad == QUADS - 2:
                    act.wait_ge(arg_ready, 1)
                    nc.scalar.activation(sm[:, 3, :], sm[:, 1, :], ACT.Ln, bias=1.0, scale=1.0) \
                        .then_inc(logs_ready, 1)
                    nc.scalar.activation(sm[:, 2, :], sm[:, 1, :], ACT.Ln, bias=1.0, scale=-1.0) \
                        .then_inc(logs_ready, 1)
            keep(QUADS - 1)

            def keep_sums(g, j):
                if j == 0:
                    act.wait_ge(merged, g + 1)
                act.wait_ge(summed, g * OCT + (j + 1 + FREE))
                nc.scalar.copy(kept[:, j, :], po[:, j % 2, 0:D]).then_inc(sums_kept, 1)

            def polish(g, part):
                if part == 0:
                    act.wait_ge(o_ready, g)
                    nc.scalar.activation(eo[:, :, :], o[:, :, :], ACT.Sigmoid).then_inc(sigmoid_ready, 1)
                elif part == 1:
                    act.wait_ge(silu_ready, g)
                    nc.scalar.activation(eo[:, :, :], o[:, :, :], ACT.Square).then_inc(o_squared, 1)
                elif part == 2:
                    act.wait_ge(norms_ready, g)
                    nc.scalar.activation(root8[:, :], nrm[:, :], ACT.Sqrt).then_inc(norms_rooted, 1)
                elif part == 3:
                    act.wait_ge(norms_kept, g)
                    nc.scalar.activation(tanh8[:, :], norm8[:, :], ACT.Tanh).then_inc(tanh_ready, 1)
                else:
                    act.wait_ge(out_ready, g)
                    act.dma_start(out_t[:, bass.ds((g - 1) * OCT, OCT), :], X[:, bass.ds((g - 1) * OCT, OCT), :]) \
                        .then_inc(out_stored, 16)

            def scales(g):
                act.wait_ge(maxima_ready, g + 1)
                nc.scalar.activation(c12[:, :, :, :], m12[:, :, :, :], ACT.Exp).then_inc(scales_ready, 1)

            def octet(g, first):
                for j in range(OCT):
                    t = g * OCT + j
                    act.wait_ge(logits_ready, t + 1)
                    nc.scalar.activation(prob[:, j % 2, :, :], lg[:, j % 2, :, :], ACT.Exp).then_inc(probs_ready, 1)
                    if j > 1:
                        keep_sums(g, j - 1)
                    ahead = (t + AHEAD + 1, (j + AHEAD + 1) % 2, False)
                    if exists(t + AHEAD + 1):
                        sign(*ahead, range(NCH // 2))
                    if j == 0 and not first:
                        scales(g - 1)
                    if exists(t + AHEAD + 1):
                        sign(*ahead, range(NCH // 2, NCH))
                    if j == 1:
                        keep_sums(g, 0)
                    if not first and j in POLISH_ACT:
                        polish(g, POLISH_ACT.index(j))
                    if j == 3:
                        for h in range(2):
                            act.wait_ge(place_turned, g * 2 + (h + 1))
                            nc.scalar.copy(placeT[:, 4 * h:4 * h + 4, :].rearrange("p t e -> p (t e)"),
                                           pt[:, 0, :]).then_inc(placeT_ready, 1)
                keep_sums(g, OCT - 1)
                act.wait_ge(vlogits_ready, g + 1)
                nc.scalar.activation(vprob[:, :, :], vlg[:, :, :], ACT.Exp).then_inc(vprobs_ready, 1)

            act.nop(nofuse=True).then_inc(sums_kept, FREE)
            for t in range(QUADS // NCH, AHEAD + 1):
                sign(t, t % 2)
            octet(0, True)
            with act.Fori(1, T // OCT - 2) as g:
                octet(g, False)
            octet(T // OCT - 2, False)
            octet(T // OCT - 1, False)
            scales(T // OCT - 1)
            for n in range(len(POLISH)):
                polish(T // OCT, n)
            with act.If(any_flagged(act) > 0):
                with act.Fori(0, T) as t:
                    flag, rank, base = control(act, t)
                    with act.If(flag > 0):
                        count = round_count(act, t, rank)
                        for r in round_loop(act, count):
                            with act.If(r < count):
                                act.wait_ge(round_logits, base + r + 1)
                                nc.scalar.activation(prob8[:, :, :], lg8[:, :, :], ACT.Exp).then_inc(round_probs, 1)
                        act.wait_ge(slow_o, rank + 1)
                        nc.scalar.activation(eo[:, 0, :], o[:, 0, :], ACT.Sigmoid).then_inc(slow_sigmoid, 1)
                        act.wait_ge(slow_nrm, rank + 1)
                        nc.scalar.activation(root8[:, 0:1], nrm[:, 0:1], ACT.Sqrt).then_inc(slow_root, 1)
                        act.wait_ge(slow_norm, rank + 1)
                        nc.scalar.activation(tanh8[:, 0:1], norm8[:, 0:1], ACT.Tanh).then_inc(slow_tanh, 1)

        @block.tensor
        def _(pe):
            pe.wait_ge(w_landed, 16 * 5)
            nc.tensor.transpose(pt[:, 0, 0:P], wraw[:, :], ident[:, :]).then_inc(w_turned, 1)
            pe.wait_ge(a_spread, 1)
            nc.tensor.matmul(pt[:, 1, 0:2 * HEADS], wraw[:, :], ablk[:, :], start=True, stop=True) \
                .then_inc(w_turned, 1)
            pe.wait_ge(waug_ready, 1)

            pe.nop(nofuse=True).then_inc(summed, FREE)
            pe.nop(nofuse=True).then_inc(vsummed, 1)

            def turn(quad, b, first):
                pe.wait_ge(relu_ready, quad // (PIECE // 4) + 1)
                if not first:
                    pe.wait_ge(rT_ready, quad - 1)
                for j in range(4):
                    tt = (quad % (PIECE // 4)) * 4 + j
                    last = nc.tensor.transpose(pt[:, b, j * P:(j + 1) * P],
                                               centred_piece(quad // (PIECE // 4) % 2)[:, tt, :], ident[:, :])
                last.then_inc(turned, 1)

            def project(quad, b):
                pe.wait_ge(rT_ready, quad + 1)
                if quad:
                    pe.wait_ge(h_read, quad)
                for j in range(4):
                    last = nc.tensor.matmul(po[:, j // 2, (j % 2) * RW:(j % 2 + 1) * RW],
                                            rT[:, b, j * P:(j + 1) * P], waug[:, :], start=True, stop=True)
                last.then_inc(h_done, 1)

            def pack(t, b, chunks=range(NCH)):
                if 0 in chunks:
                    if not isinstance(t, int) or t >= 2:
                        pe.wait_ge(keys_read, t - 1)
                    for half in range(WORDS // 512):
                        nc.tensor.matmul(keys[:, b, half * 512:(half + 1) * 512], onesrow[:, :],
                                         posrow[:, half * 512:(half + 1) * 512], start=True, stop=False)
                for c in chunks:
                    pe.wait_ge(signed, t * NCH + (c + 1))
                    for k in range(BPC):
                        for half in range(WORDS // 512):
                            at = k * WORDS + half * 512
                            last = nc.tensor.matmul(keys[:, b, half * 512:(half + 1) * 512],
                                                    packw[:, c * BPC + k, :], signs[:, c, at:at + 512],
                                                    start=False, stop=(c * BPC + k == BITS - 1))
                    last.then_inc(packed, 1)

            turn(0, 0, True)
            for quad in range(QUADS):
                if quad + 1 < QUADS:
                    turn(quad + 1, (quad + 1) % 2, quad + 1 < 2)
                project(quad, quad % 2)
                if quad == 0:
                    pe.wait_ge(const_landed, 16 * 8)
                pack(quad // NCH, quad // NCH % 2, (quad % NCH,))
            pe.wait_ge(h_read, QUADS)

            def sums(t, b, r):
                pe.wait_ge(sums_kept, t + (FREE - 1))
                pe.wait_ge(weighted, t + 1)
                for k in range(NEAR):
                    nc.tensor.matmul(po[:, b, 0:D], ident[:, :], G[:, r, k, 0:D], start=(k == 0), stop=False)
                nc.tensor.matmul(po[:, b, 0:D], ident[:, :], selfp[:, b, :], start=False, stop=True) \
                    .then_inc(summed, 1)

            def ranks(g):
                pe.wait_ge(merged, g + 1)
                pe.wait_ge(more_made, g * 2 + 2)
                nc.tensor.matmul(pt[:, 1, 0:OCT], ltri[:, :], more[:, :], start=True, stop=False)
                for j in range(OCT - 1):
                    nc.tensor.matmul(pt[:, 1, j + 1:OCT], allones[:, :],
                                     more[:, j:j + 1].broadcast_to([P, OCT - 1 - j]), start=False, stop=False)
                nc.tensor.matmul(pt[:, 1, 0:OCT], allones[:, :], zeros[:, :], start=False, stop=True) \
                    .then_inc(ranked, 1)

            def overflow_lists(g):
                pe.wait_ge(placed, g + 1)
                for j in range(OCT):
                    last = nc.tensor.matmul(pt[:, 1, 16:16 + OVER + HEADS], place[:, j, :], far[:, j, :],
                                            start=(j == 0), stop=(j == OCT - 1))
                last.then_inc(far_moved, 1)
                for h in range(2):
                    if h:
                        pe.wait_ge(placeT_ready, g * 2 + 1)
                    for j in range(4):
                        last = nc.tensor.transpose(pt[:, 0, j * P:(j + 1) * P], place[:, 4 * h + j, :], ident[:, :])
                    last.then_inc(place_turned, 1)

            def overflow_sums(g):
                pe.wait_ge(placeT_ready, g * 2 + 2)
                pe.wait_ge(vweighted, g + 1)
                for k in range(OVER):
                    last = nc.tensor.matmul(pt[:, 0, 0:D], ident[:, :], GV[:, k, 0:D], start=(k == 0),
                                            stop=(k == OVER - 1))
                last.then_inc(vsummed, 1)

            def send_back(g):
                pe.wait_ge(vres_ready, g + 1)
                pe.wait_ge(sums_kept, g * OCT + (OCT + FREE))
                for j in range(OCT):
                    nc.tensor.matmul(po[:, 1, j * 2 * HEADS:(j + 1) * 2 * HEADS], placeT[:, j, :],
                                     vres[:, D:D + 2 * HEADS], start=True, stop=True)
                for j in range(OCT):
                    last = nc.tensor.matmul(pt[:, j // 4, (j % 4) * D:(j % 4 + 1) * D], placeT[:, j, :], vres[:, 0:D],
                                            start=True, stop=True)
                last.then_inc(sent_back, 1)

            def octet(g, first):
                for j in range(OCT):
                    if j == 0 and not first:
                        send_back(g - 1)
                    if j == 1 and not first:
                        pe.wait_ge(back_kept, g)
                    sums(g * OCT + j, j % 2, j % RING)
                    if exists(g * OCT + (j + AHEAD + 1)):
                        pack(g * OCT + (j + AHEAD + 1), (j + AHEAD + 1) % 2)
                    if j == 2:
                        ranks(g)
                    if j == 3:
                        overflow_lists(g)
                overflow_sums(g)

            for t in range(QUADS // NCH, AHEAD + 1):
                pack(t, t % 2)

            octet(0, True)
            with pe.Fori(1, T // OCT - 2) as g:
                octet(g, False)
            octet(T // OCT - 2, False)
            octet(T // OCT - 1, False)
            send_back(T // OCT - 1)

            pe.wait_ge(main_done, 1)
            nc.tensor.matmul(po[0:1, 0, 0:T], ones[:, :], rowflag[:, :], start=True, stop=True) \
                .then_inc(flags_counted, 1)
            with pe.If(any_flagged(pe) > 0):
                with pe.Fori(0, T) as t:
                    flag, rank, _ = control(pe, t)
                    with pe.If(flag > 0):
                        pe.wait_ge(degrees_ready, rank + 1)
                        nc.tensor.matmul(po[0:1, 1, 0:P], degree[:, :], ident[:, :], start=True, stop=True) \
                            .then_inc(degrees_turned, 1)

        @block.vector
        def _(dve):
            V = nc.vector
            V.memset(zeros[:, :], 0.0)
            V.memset(neg_tiny[:, :], -1.1754944e-38).then_inc(tiny_set, 1)
            st = Steps(dve, prep_step)
            dve.wait_ge(w_landed, 16 * 5)
            V.tensor_scalar(ablk[:, 0:HEADS], headsel[:, :], acol[:, 0:1], None, ALU.mult)
            V.tensor_scalar(ablk[:, HEADS:2 * HEADS], headsel[:, :], acol[:, 1:2], None, ALU.mult) \
                .then_inc(a_spread, 1)
            dve.wait_ge(w_turned, 2)
            V.tensor_copy(waug[:, 0:D], pt[:, 0, 0:P])
            V.tensor_copy(waug[:, D:RW], pt[:, 1, 0:2 * HEADS]).then_inc(waug_ready, 1)
            dve.wait_ge(cleared, 1)

            def topk(steps, dst, src, spare, imm):
                for phase in range(2 * ROUNDS - 1):
                    before = steps.base + steps.n
                    r = phase // 2
                    for i in range(4):
                        if phase and i == 0:
                            dve.wait_ge(steps.sem, before - 1)
                            dve.nop(nofuse=True)
                        elif i == (3 if phase else 0):
                            dve.wait_ge(steps.sem, before)
                            dve.nop(nofuse=True)
                        if phase % 2 == 0:
                            steps.done(V.max(dst[:, i, 8 * r:8 * r + 8], src[:, i, :]))
                        else:
                            steps.done(V.match_replace(spare[:, i, :], dst[:, i, 8 * r:8 * r + 8], src[:, i, :], imm))
                    if phase % 2:
                        src = spare

            def extract(t, i, b):
                dve.wait_ge(packed, t * NCH + NCH)
                dve.nop(nofuse=True)
                for s in range(NSEG):
                    last = V.max(cand[:, i, 8 * s:8 * s + 8], keys[:, b, s * SEG:(s + 1) * SEG])
                last.then_inc(keys_read, 1)

            def decode_words(quad):
                dec = Steps(dve, dec_step, quad * N_DEC)
                dve.wait_ge(keys_read, quad * 4 + 4)
                dec.done(V.tensor_reduce(over4[:, :, 0:1], cand[:, :, 7:CANDS:8], AX, ALU.max))
                topk(dec, words, cand, cand2, -1.0)
                assert dec.n == N_WORDS, dec.n

            def decode_lists(quad, q, at):
                dec = Steps(dve, dec_step, quad * N_DEC)
                dec.n = N_WORDS

                def step(ins):
                    dec.done(ins)
                    dec.wait()

                dec.wait()
                step(V.tensor_scalar(keyi[:, :, :], words[:, :, :], float(WORDS), None, ALU.mult))
                dec.done(V.tensor_scalar(posi[:, :, :], keyi[:, :, :], WORDS - 1, None, ALU.bitwise_and))
                step(V.tensor_scalar(wi[:, :, :], keyi[:, :, :], WORDS.bit_length() - 1, None,
                                     ALU.logical_shift_right))
                step(V.tensor_copy(wf[:, :, :], wi[:, :, :]))
                for r in range(PEEL):
                    bits = wf[:, :, :].bitcast(I32)
                    dec.done(V.tensor_scalar(topbit[:, :, :], bits, 0x7F800000, None, ALU.bitwise_and))
                    step(V.tensor_scalar(bitno[:, :, :], bits, 23, WORDS.bit_length() - 1,
                                         ALU.logical_shift_right, ALU.logical_shift_left))
                    dec.done(V.tensor_tensor(ents[:, :, r * SLOTS:(r + 1) * SLOTS], bitno[:, :, :], posi[:, :, :],
                                             ALU.add))
                    step(V.tensor_tensor(wf[:, :, :], wf[:, :, :], topbit[:, :, :].bitcast(F32), ALU.subtract))
                step(V.tensor_scalar(ents[:, :, :], ents[:, :, :], 1.0 - EXPO, None, ALU.add))
                for i in range(4):
                    dec.done(V.scalar_tensor_tensor(ents[:, i, :], ents[:, i, :], selfid[:, bass.ds(quad * 4 + i, 1)],
                                                    ents[:, i, :], ALU.not_equal, ALU.mult))
                topk(dec, top, ents, ents2, -2.0 * EXPO)
                dec.done(V.tensor_reduce(over4[:, :, 2:3], wf[:, :, :], AX, ALU.max))
                dec.done(V.tensor_copy(over4[:, :, 1:2], words[:, :, SLOTS - 1:SLOTS]))
                dec.wait()
                dec.done(V.tensor_copy(over4[:, :, 3:4], top[:, :, SLOTS - 1:SLOTS]))
                dec.done(V.tensor_scalar(topc[:, :, :], top[:, :, :], 0.0, None, ALU.max))
                dec.done(V.tensor_scalar(inv[:, :, :], top[:, :, :], 0.5, None, ALU.is_lt))
                dec.wait()
                dec.done(V.scalar_tensor_tensor(idxf[:, :, :], inv[:, :, 0:NEAR], float(N + 1), topc[:, :, 0:NEAR],
                                                ALU.mult, ALU.add))
                step(V.tensor_scalar(pen[:, :, :], inv[:, :, 0:NEAR], NEG, None, ALU.mult))
                V.tensor_scalar(idx[:, q, :, :], idxf[:, :, :], -1.0, None, ALU.add).then_inc(lists_ready, 1)
                e_l = H[:, bass.ds(quad * 4, 4), ROW:RW]
                dec.done(V.tensor_copy(maskel[:, q, :, :, :], e_l.unsqueeze(2).broadcast_to([P, 4, NEAR, HEADS])))
                dec.done(V.tensor_reduce(over[:, bass.ds(quad * 4, 4)], over4[:, :, :], AX, ALU.max))
                dec.done(V.tensor_copy(far[:, at:at + 4, 0:OVER], topc[:, :, NEAR:SLOTS]))
                dec.done(V.tensor_copy(far[:, at:at + 4, OVER:OVER + HEADS], e_l))
                V.tensor_scalar(moref[:, at:at + 4], top[:, :, NEAR], 0.5, None, ALU.is_gt)
                V.tensor_scalar(more[:, at:at + 4], top[:, :, NEAR], 0.5, None, ALU.is_gt).then_inc(more_made, 1)
                dec.wait()
                flatel = maskel[:, q, :, :, :].rearrange("p t k h -> p (t k) h")
                step(V.tensor_tensor(flatel, flatel, along(pen[:, :, :].rearrange("p t k -> p (t k)"), HEADS),
                                     ALU.add))
                assert dec.n == N_DEC, dec.n

            def means(i):
                here = slice(i * PIECE, (i + 1) * PIECE)
                dve.wait_ge(x_landed[i], 16)
                st.done(V.tensor_reduce(mean[:, here], X[:, here, :], AX, ALU.add))
                st.wait()
                V.tensor_scalar(mean[:, here], mean[:, here], 1.0 / D, None, ALU.mult).then_inc(means_ready, 1)

            def stats(i):
                here = slice(i * PIECE, (i + 1) * PIECE)
                piece = centred_piece(i % 2)
                dve.wait_ge(centred_squared, i + 1)
                V.tensor_reduce(stat[:, 0, here], squares, AX, ALU.add).then_inc(centred_summed, 1)
                V.tensor_scalar(piece, piece, 0.0, None, ALU.max).then_inc(relu_ready, 1)
                if i % 2:
                    dve.wait_ge(relu_ready, i + 1)
                    dve.wait_ge(relu_summed, i)
                    dve.wait_ge(centred_summed, i + 1)
                    V.tensor_tensor(relu_squares(i), piece, piece, ALU.mult).then_inc(relu_squared, 1)
                if i + 2 < NPIECE:
                    means(i + 2)
                dve.wait_ge(relu_squared, i + 1)
                V.tensor_reduce(stat[:, 1, here], relu_squares(i), AX, ALU.add).then_inc(relu_summed, 1)

            means(0)
            means(1)
            stats(0)
            stats(1)
            dve.nop(nofuse=True).then_inc(merged, 1)
            dve.wait_ge(const_landed, 16 * 8)
            extract(0, 0, 0)
            stats(2)
            extract(1, 1, 1)
            stats(3)

            def small(ins):
                st.done(ins)
                st.wait()

            dve.wait_ge(centred_summed, NPIECE)
            dve.wait_ge(relu_summed, NPIECE)
            V.tensor_scalar(stat[:, 0, :], stat[:, 0, :], 1.0 / D, EPS_LN, ALU.mult, ALU.add).then_inc(stat_ready, 1)
            dve.wait_ge(root_ready, 1)
            extract(2, 2, 0)
            rstd = root[:, 0, :]
            n, arg, lm, lp, a2, poly, tmp = (sm[:, k, :] for k in range(7))
            small(V.reciprocal(rstd, rstd))
            small(V.tensor_tensor(n, root[:, 1, :], rstd, ALU.mult))
            small(V.tensor_scalar(n, n, EPS_NORM, None, ALU.max))
            V.tensor_scalar(arg, n, MAX_TANH_ARG, None, ALU.min).then_inc(arg_ready, 1)
            dve.wait_ge(arg_ready, 1)
            small(V.tensor_tensor(a2, arg, arg, ALU.mult))
            small(V.tensor_scalar(poly, a2, 1.0 / 9, 1.0 / 7, ALU.mult, ALU.add))
            for c in (1.0 / 5, 1.0 / 3, 1.0):
                small(V.tensor_tensor(poly, poly, a2, ALU.mult))
                small(V.tensor_scalar(poly, poly, c, None, ALU.add))
            small(V.tensor_tensor(poly, poly, arg, ALU.mult))
            dve.wait_ge(logs_ready, 2)
            small(V.tensor_tensor(lp, lp, lm, ALU.subtract))
            small(V.tensor_scalar(lp, lp, 0.5, None, ALU.mult))
            small(V.tensor_tensor(poly, poly, lp, ALU.subtract))
            small(V.tensor_scalar(tmp, arg, 0.1, None, ALU.is_lt))
            small(V.tensor_tensor(poly, poly, tmp, ALU.mult))
            small(V.tensor_tensor(lp, lp, poly, ALU.add))
            small(V.reciprocal(n, n))
            small(V.tensor_tensor(lp, lp, n, ALU.mult))
            V.tensor_tensor(factor[:, :], lp, rstd, ALU.mult).then_inc(factors_ready, 1)
            dve.wait_ge(factors_ready, 1)
            dve.wait_ge(h_read, QUADS)
            for i in range(V_PIECES):
                here = slice(i * PIECE, (i + 1) * PIECE)
                V.tensor_tensor(H[:, here, :], H[:, here, :], along(factor[:, here], RW), ALU.mult).then_inc(scaled, 1)
            extract(3, 3, 1)
            decode_words(0)
            dve.wait_ge(scaled, V_PIECES)
            dve.wait_ge(scaled_pool, NPIECE - V_PIECES)
            small(V.tensor_tensor(selfl[:, :, :], H[:, :, D:ROW], H[:, :, ROW:RW], ALU.add))
            small(V.scalar_tensor_tensor(selfl[:, :, :], selfl[:, :, :], 0.2, selfl[:, :, :], ALU.mult, ALU.max))
            decode_lists(0, 0, 0)
            for t in range(4, AHEAD - 1):
                extract(t, t % 4, t % 2)

            def weigh_logits(g, j, at):
                t, b = g * OCT + j, j % 2
                att = Steps(dve, att_step, t * N_ATT)

                def step(ins):
                    att.done(ins)
                    att.wait()

                L = lg[:, b, :, :]
                near = L[:, 0:NEAR, :]
                att.done(V.tensor_copy(L[:, NEAR:NEAR + 1, :], selfl[:, bass.ds(t, 1), :]))
                dve.wait_ge(gathered[j % RING], g * (RING * 16 * NEAR) + (j // RING + 1) * 16 * NEAR)
                step(V.tensor_tensor(near, G[:, j % RING, :, D:ROW], maskel[:, j // 4, j % 4, :, :], ALU.add))
                step(V.scalar_tensor_tensor(near, near, 0.2, near, ALU.mult, ALU.max))
                step(V.tensor_reduce(rowmax[:, at, :], L.rearrange("p k h -> p h k"), AX, ALU.max))
                V.tensor_tensor(L, L, rowmax[:, at:at + 1, :].broadcast_to([P, NEAR + 1, HEADS]),
                                ALU.subtract).then_inc(logits_ready, 1)
                assert att.n == N_ATT

            def weigh_rows(g, j, at):
                t, b = g * OCT + j, j % 2
                dve.wait_ge(probs_ready, t + 1)
                pr = prob[:, b, :, :]
                dve.wait_ge(summed, t + (FREE - 1))
                rows = G[:, j % RING, :, 0:D].rearrange("p k (h d) -> p k h d", h=HEADS)
                V.tensor_tensor(rows, rows, pr[:, 0:NEAR, :].unsqueeze(3)
                                .broadcast_to([P, NEAR, HEADS, HD]), ALU.mult)
                V.tensor_tensor(selfp[:, b, :].rearrange("p (h d) -> p h d", h=HEADS),
                                H[:, bass.ds(t, 1), 0:D].rearrange("p u (h d) -> p (u h) d", h=HEADS),
                                along(pr[:, NEAR, :], HD), ALU.mult).then_inc(weighted, 1)
                V.tensor_reduce(den[:, at, :], pr.rearrange("p k h -> p h k"), AX, ALU.add).then_inc(dens_made, 1)

            def overflow_lists(g):
                vl = Steps(dve, vl_step, g * N_VL)

                def step(ins):
                    vl.done(ins)
                    vl.wait()

                vl.done(V.tensor_scalar(nomore[:, :], moref[:, :], -1.0, -NEG, ALU.add, ALU.mult))
                dve.wait_ge(ranked, g + 1)
                step(V.tensor_scalar(dest[:, :], moref[:, :], -4.0 * N, 4.0 * N, ALU.mult, ALU.add))
                step(V.tensor_tensor(dest[:, :], dest[:, :], pt[:, 1, 0:OCT], ALU.add))
                step(V.scalar_tensor_tensor(lost[:, :], dest[:, :], P - 0.5, moref[:, :], ALU.is_gt, ALU.mult))
                flags = over[:, bass.ds(g * OCT, OCT)]
                vl.done(V.tensor_tensor(flags, flags, lost[:, :], ALU.max))
                for j in range(OCT):
                    last = V.tensor_scalar(place[:, j, :], iota_e[:, :], dest[:, j:j + 1], None, ALU.is_equal)
                last.then_inc(placed, 1)

            def overflow_entries(g):
                vl = Steps(dve, vl_step, g * N_VL)
                vl.n = 5

                def step(ins):
                    vl.done(ins)
                    vl.wait()

                dve.wait_ge(far_moved, g + 1)
                step(V.tensor_copy(vfar[:, :], pt[:, 1, 16:16 + OVER + HEADS]))
                step(V.tensor_scalar(vinv[:, :], vfar[:, 0:OVER], 0.5, None, ALU.is_lt))
                vl.done(V.tensor_scalar(vpen[:, :], vinv[:, :], NEG, None, ALU.mult))
                step(V.scalar_tensor_tensor(vidxf[:, :], vinv[:, :], float(N + 1), vfar[:, 0:OVER], ALU.mult, ALU.add))
                V.tensor_scalar(vidx[:, :], vidxf[:, :], -1.0, None, ALU.add).then_inc(vlists_ready, 1)
                vl.done(V.tensor_tensor(vmaskel[:, :, :], along(vpen[:, :], HEADS),
                                        vfar[:, OVER:OVER + HEADS].unsqueeze(1).broadcast_to([P, OVER, HEADS]),
                                        ALU.add))
                assert vl.n == N_VL, vl.n

            def overflow_weigh(g):
                va = Steps(dve, vatt_step, g * N_VATT)

                def step(ins):
                    va.done(ins)
                    va.wait()

                dve.wait_ge(gathered[OCT % RING], g * (RING * 16 * NEAR) + RING * 16 * NEAR)
                dve.wait_ge(vl_step, g * N_VL + N_VL)
                step(V.tensor_tensor(vlg[:, :, :], GV[:, :, D:ROW], vmaskel[:, :, :], ALU.add))
                Lf = vlg[:, :, :].rearrange("p k h -> p (k h)")
                step(V.scalar_tensor_tensor(Lf, Lf, 0.2, Lf, ALU.mult, ALU.max))
                vmax = vres[:, D + HEADS:D + 2 * HEADS]
                step(V.tensor_reduce(vmax, vlg[:, :, :].rearrange("p k h -> p h k"), AX, ALU.max))
                V.tensor_tensor(vlg[:, :, :], vlg[:, :, :], vmax.unsqueeze(1).broadcast_to([P, OVER, HEADS]),
                                ALU.subtract).then_inc(vlogits_ready, 1)
                dve.wait_ge(vprobs_ready, g + 1)
                rows = GV[:, :, 0:D].rearrange("p k (h d) -> p k h d", h=HEADS)
                V.tensor_tensor(rows, rows, vprob[:, :, :].unsqueeze(3).broadcast_to([P, OVER, HEADS, HD]),
                                ALU.mult).then_inc(vweighted, 1)
                va.done(V.tensor_reduce(vres[:, D:D + HEADS], vprob[:, :, :].rearrange("p k h -> p h k"), AX,
                                        ALU.add))
                assert va.n == N_VATT, va.n

            def overflow_done(g):
                dve.wait_ge(vatt_step, g * N_VATT + N_VATT)
                dve.wait_ge(vsummed, g + 2)
                V.tensor_copy(vres[:, 0:D], pt[:, 0, 0:D]).then_inc(vres_ready, 1)

            def flat(ap):
                return ap.rearrange("p t h -> p (t h)")

            m1, m2 = m12[:, 0, :, :], m12[:, 1, :, :]
            c1, c2 = c12[:, 0, :, :], c12[:, 1, :, :]
            N_MAXIMA = 2

            def merge_maxima(g):
                me = Steps(dve, merge_step, g * N_MERGE)

                def step(ins):
                    me.done(ins)
                    me.wait()

                dve.wait_ge(sent_back, g + 1)
                V.tensor_copy(back[:, :, :], po[:, 1, 0:OCT * 2 * HEADS].rearrange("p (t c) -> p t c", c=2 * HEADS)) \
                    .then_inc(back_kept, 1)
                dve.wait_ge(back_kept, g + 1)
                step(V.tensor_tensor(m2, back[:, :, HEADS:2 * HEADS], along(nomore[:, :], HEADS), ALU.add))
                step(V.tensor_tensor(allmax[:, :, :], rowmax[:, 0:OCT, :], m2, ALU.max))
                V.tensor_tensor(m1, rowmax[:, 0:OCT, :], allmax[:, :, :], ALU.subtract)
                V.tensor_tensor(m2, m2, allmax[:, :, :], ALU.subtract).then_inc(maxima_ready, 1)
                assert me.n == N_MAXIMA

            def merge(g):
                me = Steps(dve, merge_step, g * N_MERGE)
                me.n = N_MAXIMA

                def step(ins):
                    me.done(ins)
                    me.wait()

                def heads(ap):
                    return ap.rearrange("p t (h d) -> p (t h) d", h=HEADS)

                dens = den[:, 0:OCT, :]
                dve.wait_ge(scales_ready, g + 1)
                me.done(V.tensor_tensor(allden[:, :, :], back[:, :, 0:HEADS], c2, ALU.mult))
                step(V.tensor_tensor(dens, dens, c1, ALU.mult))
                step(V.tensor_tensor(allden[:, :, :], allden[:, :, :], dens, ALU.add))
                step(V.reciprocal(allden[:, :, :], allden[:, :, :]))
                me.done(V.tensor_tensor(c1, c1, allden[:, :, :], ALU.mult))
                step(V.tensor_tensor(c2, c2, allden[:, :, :], ALU.mult))
                me.done(V.tensor_tensor(heads(kept[:, :, :]), heads(kept[:, :, :]), along(flat(c1), HD), ALU.mult))
                me.done(V.tensor_tensor(heads(o[:, :, :]), pt[:, :, :].rearrange("p b (c d) -> p (b c) d", d=HD),
                                        along(flat(c2), HD), ALU.mult))
                me.wait()
                V.tensor_tensor(o[:, :, :], o[:, :, :], kept[:, :, :], ALU.add).then_inc(merged, 1)
                assert me.n == N_MERGE, me.n

            def polish(g, part):
                pol = Steps(dve, pol_step, (g - 1) * N_POL)
                pol.n = (0, 0, 1, 1, 3)[part]

                def step(ins):
                    pol.done(ins)
                    pol.wait()

                if part == 0:
                    dve.wait_ge(merged, g + 1)
                    V.tensor_tensor(o[:, :, :], o[:, :, :], biasb[:, :].unsqueeze(1).broadcast_to([P, OCT, D]),
                                    ALU.add).then_inc(o_ready, 1)
                elif part == 1:
                    dve.wait_ge(sigmoid_ready, g)
                    pol.done(V.tensor_tensor(o[:, :, :], o[:, :, :], eo[:, :, :], ALU.mult))
                    pol.wait()
                    dve.nop(nofuse=True).then_inc(silu_ready, 1)
                elif part == 2:
                    dve.wait_ge(o_squared, g)
                    V.tensor_reduce(nrm[:, :], eo[:, :, :], AX, ALU.add).then_inc(norms_ready, 1)
                elif part == 3:
                    dve.wait_ge(norms_rooted, g)
                    step(V.tensor_scalar(norm8[:, :], root8[:, :], EPS_NORM, None, ALU.max))
                    dve.nop(nofuse=True).then_inc(norms_kept, 1)
                    pol.done(V.reciprocal(scale8[:, :], norm8[:, :]))
                    pol.wait()
                else:
                    dve.wait_ge(tanh_ready, g)
                    step(V.tensor_tensor(scale8[:, :], scale8[:, :], tanh8[:, :], ALU.mult))
                    step(V.tensor_tensor(o[:, :, :], o[:, :, :], along(scale8[:, :], D), ALU.mult))
                    xs = X[:, bass.ds((g - 1) * OCT, OCT), :]
                    step(V.tensor_tensor(xs, xs, o[:, :, :], ALU.add))
                    dve.nop(nofuse=True).then_inc(out_ready, 1)
                    assert pol.n == N_POL, pol.n

            def octet(g, first, last):
                for j in range(OCT):
                    t = g * OCT + j
                    weigh_logits(g, j, OCT if not first and j == 0 else j)
                    if not first and j == 0:
                        overflow_done(g - 1)
                    weigh_rows(g, j, OCT + j if not first and j < 2 else j)
                    if first and j == 0:
                        extract(AHEAD - 1, (AHEAD - 1) % 4, (AHEAD - 1) % 2)
                        decode_words(1)
                    if not last:
                        extract(t + AHEAD, (j + AHEAD) % 4, (j + AHEAD) % 2)
                    if not first and j == 0:
                        merge_maxima(g - 1)
                        dve.wait_ge(maxima_ready, g)
                        V.tensor_copy(rowmax[:, 0, :], rowmax[:, OCT, :])
                    if not first and j == 1:
                        merge(g - 1)
                        V.tensor_copy(den[:, 0:2, :], den[:, OCT:OCT + 2, :])
                    if not first and j in POLISH:
                        polish(g, POLISH.index(j))
                    if j == 3:
                        overflow_lists(g)
                    if j == 4:
                        overflow_entries(g)
                    if j == 0:
                        decode_lists(g * 2 + 1, 1, 4)
                    if j == 4 and not last:
                        decode_lists(g * 2 + 2, 0, 0)
                    if j % 4 == 3 and not last:
                        decode_words(g * 2 + (j // 4 + 2))
                overflow_weigh(g)

            octet(0, True, False)
            with dve.Fori(1, T // OCT - 1) as g:
                octet(g, False, False)
            octet(T // OCT - 1, False, True)
            overflow_done(T // OCT - 1)
            merge_maxima(T // OCT - 1)
            merge(T // OCT - 1)
            for n in range(len(POLISH)):
                polish(T // OCT, n)

            fl = Steps(dve, flags_step)

            def flagstep(ins):
                fl.done(ins)
                fl.wait()

            V.memset(ones[:, :], 1.0)
            V.tensor_scalar(rowflag[:, :], over[:, :], 1.0, None, ALU.is_ge).then_inc(main_done, 1)
            dve.wait_ge(flags_counted, 1)
            flagstep(V.tensor_scalar(flagrow[:, :], po[0:1, 0, 0:T], 0.5, None, ALU.is_gt))
            flagstep(V.tensor_reduce(anyflag[:, :], flagrow[:, :], AX, ALU.add))
            V.tensor_copy(anyi[:, :], anyflag[:, :]).then_inc(any_ready, 1)

            def slow_tile(t, rank, base):
                SLOW, ROUND, SLOW_TAIL = 12, 19, 6
                sl = Steps(dve, slow_step, rank * SLOW, apart=True)

                def step(ins):
                    sl.done(ins)
                    sl.wait()

                heads = "p (h d) -> p h d"
                e_l = H[:, bass.ds(t, 1), ROW:RW]
                dve.wait_ge(slow_adj, rank * 48 + 48)
                step(V.scalar_tensor_tensor(slow_keys, slow_keys, 0.0, colid, ALU.is_gt, ALU.mult))
                step(V.scalar_tensor_tensor(slow_keys, colid, selfid[:, bass.ds(t, 1)], slow_keys, ALU.not_equal,
                                            ALU.mult))
                V.tensor_scalar(signs[:, :, :].rearrange("p c n -> p (c n)"), slow_keys, 0.5, None, ALU.is_gt,
                                ALU.add, accum_out=degree[:, :]).then_inc(degrees_ready, 1)
                dve.wait_ge(degrees_turned, rank + 1)
                step(V.tensor_reduce(maxdeg[:, :], po[0:1, 1, 0:P], AX, ALU.max))
                step(V.tensor_scalar(degi[:, :], maxdeg[:, :], 7.0, None, ALU.add))
                step(V.tensor_scalar(rounds[0:1, bass.ds(t, 1)], degi[:, :], 3, None, ALU.logical_shift_right))
                step(V.tensor_copy(maxdeg[:, :], rounds[0:1, bass.ds(t, 1)]))
                step(V.tensor_tensor(tally[0:1, bass.ds(t + 1, 1), 1], tally[0:1, bass.ds(t + 1, 1), 1], maxdeg[:, :],
                                     ALU.add))
                step(V.tensor_tensor(oldmax[:, :], slow_own[:, D:ROW], e_l[:, 0, :], ALU.add))
                step(V.scalar_tensor_tensor(oldmax[:, :], oldmax[:, :], 0.2, oldmax[:, :], ALU.mult, ALU.max))
                sl.done(V.memset(den8[:, :], 1.0))
                V.tensor_copy(acc[:, :], slow_own[:, 0:D]).then_inc(rounds_ready, 1)
                count = round_count(dve, t, rank)
                for r in round_loop(dve, count):
                    with dve.If(r < count):
                        n = base + r
                        rs = Steps(dve, round_step, n * ROUND, apart=True)

                        def rstep(ins):
                            rs.done(ins)
                            rs.wait()

                        rstep(V.max(top8[:, :], slow_keys))
                        dve.nop(nofuse=True)
                        rs.done(V.match_replace(slow_keys, top8[:, :], slow_keys, 0.0))
                        rstep(V.tensor_scalar(inv8[:, :], top8[:, :], 0.5, None, ALU.is_lt))
                        rs.done(V.tensor_scalar(pen8[:, :], inv8[:, :], NEG, None, ALU.mult))
                        rstep(V.scalar_tensor_tensor(idxf8[:, :], inv8[:, :], float(N + 1), top8[:, :], ALU.mult,
                                                     ALU.add))
                        V.tensor_scalar(idx8[:, :], idxf8[:, :], -1.0, None, ALU.add).then_inc(round_lists, 1)
                        dve.wait_ge(round_gathered, n * 128 + 128)
                        L = lg8[:, 0:8, :]
                        rstep(V.tensor_tensor(L, G[:, 0, 0:8, D:ROW], e_l.broadcast_to([P, 8, HEADS]), ALU.add))
                        rstep(V.scalar_tensor_tensor(L, L, 0.2, L, ALU.mult, ALU.max))
                        rstep(V.tensor_tensor(L, L, along(pen8[:, :], HEADS), ALU.add))
                        rstep(V.tensor_reduce(rmax8[:, :], L.rearrange("p k h -> p h k"), AX, ALU.max))
                        rs.done(V.tensor_tensor(newmax[:, :], oldmax[:, :], rmax8[:, :], ALU.max))
                        rstep(V.tensor_copy(lg8[:, 8, :], oldmax[:, :]))
                        V.tensor_tensor(lg8[:, :, :], lg8[:, :, :],
                                        newmax[:, :].unsqueeze(1).broadcast_to([P, 9, HEADS]),
                                        ALU.subtract).then_inc(round_logits, 1)
                        rs.done(V.tensor_copy(oldmax[:, :], newmax[:, :]))
                        dve.wait_ge(round_probs, n + 1)
                        rs.done(V.tensor_reduce(sum8[:, :], prob8[:, 0:8, :].rearrange("p k h -> p h k"), AX,
                                                ALU.add))
                        rstep(V.tensor_tensor(den8[:, :], den8[:, :], prob8[:, 8, :], ALU.mult))
                        rs.done(V.tensor_tensor(den8[:, :], den8[:, :], sum8[:, :], ALU.add))
                        rows = G[:, 0, 0:8, 0:D].rearrange("p k (h d) -> p k h d", h=HEADS)
                        rstep(V.tensor_tensor(rows, rows, prob8[:, 0:8, :].unsqueeze(3)
                                              .broadcast_to([P, 8, HEADS, HD]), ALU.mult))
                        rs.done(V.tensor_reduce(part[:, :], G[:, 0, 0:8, 0:D].rearrange("p k d -> p d k"), AX,
                                                ALU.add))
                        av = acc[:, :].rearrange(heads, h=HEADS)
                        rstep(V.tensor_tensor(av, av, along(prob8[:, 8, :], HD), ALU.mult))
                        rstep(V.tensor_tensor(acc[:, :], acc[:, :], part[:, :], ALU.add))
                        assert rs.n == ROUND, rs.n
                step(V.reciprocal(den8[:, :], den8[:, :]))
                step(V.tensor_tensor(o[:, 0, :].rearrange(heads, h=HEADS), acc[:, :].rearrange(heads, h=HEADS),
                                     along(den8[:, :], HD), ALU.mult))
                V.tensor_tensor(o[:, 0, :], o[:, 0, :], biasb[:, :], ALU.add).then_inc(slow_o, 1)
                assert sl.n == SLOW, sl.n
                dve.wait_ge(slow_sigmoid, rank + 1)
                tail = Steps(dve, tail_step, rank * SLOW_TAIL, apart=True)

                def tstep(ins):
                    tail.done(ins)
                    tail.wait()

                z = o[:, 0, :]
                tstep(V.tensor_tensor(z, z, eo[:, 0, :], ALU.mult))
                tstep(V.tensor_tensor(eo[:, 1, :], z, z, ALU.mult))
                V.tensor_reduce(nrm[:, 0:1], eo[:, 1, :], AX, ALU.add).then_inc(slow_nrm, 1)
                dve.wait_ge(slow_root, rank + 1)
                V.tensor_scalar(norm8[:, 0:1], root8[:, 0:1], EPS_NORM, None, ALU.max).then_inc(slow_norm, 1)
                dve.wait_ge(slow_norm, rank + 1)
                tstep(V.reciprocal(scale8[:, 0:1], norm8[:, 0:1]))
                dve.wait_ge(slow_tanh, rank + 1)
                tstep(V.tensor_tensor(scale8[:, 0:1], scale8[:, 0:1], tanh8[:, 0:1], ALU.mult))
                tstep(V.tensor_scalar(z, z, scale8[:, 0:1], None, ALU.mult))
                tstep(V.tensor_tensor(slow_out, slow_x, z, ALU.add))
                assert tail.n == SLOW_TAIL, tail.n
                dve.nop(nofuse=True).then_inc(slow_out_ready, 1)
                dve.wait_ge(slow_stored, rank * 16 + 16)
                dve.nop(nofuse=True).then_inc(slow_free, 1)

            with dve.If(any_flagged(dve) > 0):
                fl.done(V.memset(tally[:, :, :], 0.0))
                fl.wait()
                V.drain().then_inc(slow_free, 1)
                dve.wait_ge(colid_landed, 16)
                with dve.Fori(0, T) as t:
                    tl = Steps(dve, tally_step, t * 3, apart=True)
                    tl.done(V.tensor_tensor(tally[0:1, bass.ds(t + 1, 1), 0], tally[0:1, bass.ds(t, 1), 0],
                                            flagrow[0:1, bass.ds(t, 1)], ALU.add))
                    tl.done(V.tensor_copy(tally[0:1, bass.ds(t + 1, 1), 1], tally[0:1, bass.ds(t, 1), 1]))
                    tl.done(V.tensor_copy(ctl[0:1, bass.ds(t, 1), 0], flagrow[0:1, bass.ds(t, 1)]))
                    tl.wait()
                    V.tensor_copy(ctl[0:1, bass.ds(t, 1), 1:3], tally[0:1, bass.ds(t, 1), :]).then_inc(ctl_ready, 1)
                    flag, rank, base = control(dve, t)
                    with dve.If(flag > 0):
                        slow_tile(t, rank, base)


def kernel(x, adj, L0_gnn_W, L0_gnn_a_l, L0_gnn_a_r, L0_gnn_bias):
    import numpy as np
    import ml_dtypes
    import concourse.bacc as bacc
    from concourse.bass_utils import run_bass_kernel_spmd

    N = 8192
    W = N // BITS
    pos = np.arange(W)
    packw = np.zeros((P, BITS, P), np.float32)
    packw[np.arange(P), :, np.arange(P)] = 2.0 ** (np.arange(BITS) - 1)
    consts = {
        "ident": np.eye(P, dtype=np.float32),
        "packw": packw.astype(ml_dtypes.bfloat16),
        "posrow": np.stack([np.full(W, (2 ** BITS - 1) / 2), (pos // 32 * 32) / W, (pos % 32) / W])
                  .astype(ml_dtypes.bfloat16),
        "onesrow": np.ones((3, P), ml_dtypes.bfloat16),
        "selfid": (np.arange(P)[:, None] + P * np.arange(N // P)[None, :] + 1).astype(np.float32),
        "headsel": (np.arange(P)[:, None] // (P // HEADS) == np.arange(HEADS)[None, :]).astype(np.float32),
        "colid": np.arange(1, N + 1, dtype=np.float32)[None, :],
        "ltri": np.triu(np.ones((P, P)), 1).astype(ml_dtypes.bfloat16),
        "allones": np.ones((P, P), ml_dtypes.bfloat16),
        "iota_e": np.broadcast_to(np.arange(P, dtype=np.float32), (P, P)),
    }
    nc = bacc.Bacc("TRN2", target_bir_lowering=False, num_devices=1)
    arrays = {"x": x, "adj": adj, "W": L0_gnn_W, "a_l": L0_gnn_a_l, "a_r": L0_gnn_a_r, "bias": L0_gnn_bias, **consts}
    args, feed = [], {}
    for name, a in arrays.items():
        a = np.ascontiguousarray(a)
        feed[f"in_{name}"] = a
        args.append(nc.dram_tensor(f"in_{name}", a.shape, mybir.dt.from_np(a.dtype), kind="ExternalInput").ap())
    args.append(nc.dram_tensor("out", (N, P), F32, kind="ExternalOutput").ap())
    build(nc, *args)
    r = run_bass_kernel_spmd(nc, [feed], core_ids=[0])
    return r.results[0]["out"]
```
